# Optimizing a Trainium2 kernel written in Bass

```python
import numpy as np
import jax
import jax.numpy as jnp

def _softmax(x, axis=-1):
    return jax.nn.softmax(x, axis=axis)

def _gelu(x):
    return jax.nn.gelu(x, approximate=True)

def _silu(x):
    return jax.nn.silu(x)

def _sigmoid(x):
    return jax.nn.sigmoid(x)

def _layernorm(x, axis=-1, eps=1e-05):
    m = jnp.mean(x, axis=axis, keepdims=True)
    v = jnp.var(x, axis=axis, keepdims=True)
    return (x - m) / jnp.sqrt(v + eps)

def _scatter_add(tgt, idx, src, axis=0):
    return tgt.at[idx].add(src)

def _segment_sum(src, seg, n):
    return jax.ops.segment_sum(src, seg, n)
kernel_name = 'mk_xattn_seq_d2_seqx_r8_3e03ed'

def setup_inputs(seed: int=0):
    np.random.seed(seed)
    _w = jnp.asarray

    def _rec_inputs():
        import jax
        import jax.numpy as jnp
        _rk = jax.random.key(seed)
        x = -0.0002928 + 1 * jax.random.normal(jax.random.fold_in(_rk, 1), (8, 256, 128), jnp.float32)
        _lenS = 256 - jax.random.randint(jax.random.fold_in(_rk, 7), (8,), 0, max(1, 256 // 4) + 1, jnp.int32)
        _lenS2 = 64 - jax.random.randint(jax.random.fold_in(_rk, 8), (8,), 0, max(1, 64 // 4) + 1, jnp.int32)
        _ctx_1024P = jax.random.normal(jax.random.fold_in(_rk, 11), (8, 16, 128), jnp.float32)
        _ctx_1024c = jax.random.dirichlet(jax.random.fold_in(_rk, 511), 0.3 * jnp.ones((16,), jnp.float32), (8, 64))
        _ctx_1024t = jnp.einsum('bsk,bkd->bsd', _ctx_1024c, _ctx_1024P)
        _ctx_1024t = _ctx_1024t * jax.lax.rsqrt(jnp.mean(jnp.square(_ctx_1024t)) + 1e-12) * 0.953939
        ctx_1024 = -1.39393e-06 + 0.999914 * (_ctx_1024t + 0.3 * jax.random.normal(jax.random.fold_in(_rk, 611), (8, 64, 128), jnp.float32))
        return (x, ctx_1024)
    x, ctx_1024 = _rec_inputs()

    def _L0_xattn_setup():
        import jax, jax.numpy as jnp
        import numpy as np
        B, Q, KV = (2, 256, 256)
        D_MODEL = 128
        N_HEADS = 16
        D_KV = 64
        EPS = 1e-06
        key = jax.random.key(seed)
        ks = jax.random.split(key, 7)
        s = 0.02
        return {'hidden_states': jax.random.normal(ks[0], (B, Q, D_MODEL), jnp.float32), 'key_value_states': jax.random.normal(ks[1], (B, KV, D_MODEL), jnp.float32), 'wq': jax.random.normal(ks[2], (D_MODEL, N_HEADS * D_KV), jnp.float32) * s, 'wk': jax.random.normal(ks[3], (D_MODEL, N_HEADS * D_KV), jnp.float32) * s, 'wv': jax.random.normal(ks[4], (D_MODEL, N_HEADS * D_KV), jnp.float32) * s, 'wo': jax.random.normal(ks[5], (N_HEADS * D_KV, D_MODEL), jnp.float32) * s, 'norm_w': jnp.ones((D_MODEL,), jnp.float32)}
    _L0_xattn_all = _L0_xattn_setup()
    _L0_xattn_in = {k: v for k, v in _L0_xattn_all.items() if k in ('wq', 'wk', 'wv', 'wo', 'norm_w')}
    del _L0_xattn_all

    def _L1_xattn_setup():
        import jax, jax.numpy as jnp
        import numpy as np
        B, S, SE, D, H, FF, E, K = (2, 256, 256, 128, 16, 512, 8, 2)
        HD = D // H

        def _layernorm(x, g, b):
            m = x.mean(-1, keepdims=True)
            v = ((x - m) ** 2).mean(-1, keepdims=True)
            return (x - m) / jnp.sqrt(v + 1e-05) * g + b

        def _attn(q_in, k_in, v_in, wq, bq, wk, bk, wv, bv, wo, bo, causal):
            Bq, Sq, Dm = q_in.shape
            Sk = k_in.shape[1]
            Q = (q_in @ wq + bq).reshape(Bq, Sq, H, HD)
            Kp = (k_in @ wk + bk).reshape(Bq, Sk, H, HD)
            V = (v_in @ wv + bv).reshape(Bq, Sk, H, HD)
            scores = jnp.einsum('bqhd,bkhd->bhqk', Q, Kp) / jnp.sqrt(jnp.float32(HD))
            if causal:
                mask = jnp.tril(jnp.ones((Sq, Sk), bool))
                scores = jnp.where(mask, scores, -jnp.inf)
            a = jax.nn.softmax(scores, axis=-1)
            o = jnp.einsum('bhqk,bkhd->bqhd', a, V).reshape(Bq, Sq, Dm)
            return o @ wo + bo

        def _moe(x, rw, rb, w1, b1, w2, b2):
            T = x.shape[0] * x.shape[1]
            xf = x.reshape(T, D)
            router_weights = jax.nn.softmax(xf @ rw + rb, axis=-1)
            topw, topi = jax.lax.top_k(router_weights, K)
            topw = jax.nn.softmax(topw, axis=-1)
            combine = jnp.zeros((T, E), xf.dtype).at[jnp.arange(T)[:, None], topi].add(topw)
            h = jax.nn.gelu(jnp.einsum('td,edf->etf', xf, w1) + b1[:, None, :], approximate=False)
            eo = jnp.einsum('etf,efd->etd', h, w2) + b2[:, None, :]
            out = jnp.einsum('etd,te->td', eo, combine)
            return out.reshape(x.shape)
        key = jax.random.key(seed)
        ks = jax.random.split(key, 32)
        w = lambda k, shape: jax.random.normal(k, shape, jnp.float32) * 0.02
        inp = {'x': jax.random.normal(ks[0], (B, S, D), jnp.float32), 'encoder_output': jax.random.normal(ks[1], (B, SE, D), jnp.float32), 'sa_wq': w(ks[2], (D, D)), 'sa_bq': jnp.zeros((D,), jnp.float32), 'sa_wk': w(ks[3], (D, D)), 'sa_bk': jnp.zeros((D,), jnp.float32), 'sa_wv': w(ks[4], (D, D)), 'sa_bv': jnp.zeros((D,), jnp.float32), 'sa_wo': w(ks[5], (D, D)), 'sa_bo': jnp.zeros((D,), jnp.float32), 'ca_wq': w(ks[6], (D, D)), 'ca_bq': jnp.zeros((D,), jnp.float32), 'ca_wk': w(ks[7], (D, D)), 'ca_bk': jnp.zeros((D,), jnp.float32), 'ca_wv': w(ks[8], (D, D)), 'ca_bv': jnp.zeros((D,), jnp.float32), 'ca_wo': w(ks[9], (D, D)), 'ca_bo': jnp.zeros((D,), jnp.float32), 'ln1_g': jnp.ones((D,), jnp.float32), 'ln1_b': jnp.zeros((D,), jnp.float32), 'ln2_g': jnp.ones((D,), jnp.float32), 'ln2_b': jnp.zeros((D,), jnp.float32), 'ln3_g': jnp.ones((D,), jnp.float32), 'ln3_b': jnp.zeros((D,), jnp.float32), 'router_w': w(ks[10], (D, E)), 'router_b': jnp.zeros((E,), jnp.float32), 'e_w1': w(ks[11], (E, D, FF)), 'e_b1': jnp.zeros((E, FF), jnp.float32), 'e_w2': w(ks[12], (E, FF, D)), 'e_b2': jnp.zeros((E, D), jnp.float32)}
        return inp
    _L1_xattn_all = _L1_xattn_setup()
    _L1_xattn_in = {k: v for k, v in _L1_xattn_all.items() if k in ('sa_wq', 'sa_bq', 'sa_wk', 'sa_bk', 'sa_wv', 'sa_bv', 'sa_wo', 'sa_bo', 'ca_wq', 'ca_bq', 'ca_wk', 'ca_bk', 'ca_wv', 'ca_bv', 'ca_wo', 'ca_bo', 'ln1_g', 'ln1_b', 'ln2_g', 'ln2_b', 'ln3_g', 'ln3_b', 'router_w', 'router_b', 'e_w1', 'e_b1', 'e_w2', 'e_b2')}
    del _L1_xattn_all
    return {'x': x, 'ctx_1024': ctx_1024, 'L0_xattn_wq': _L0_xattn_in['wq'], 'L0_xattn_wk': _L0_xattn_in['wk'], 'L0_xattn_wv': _L0_xattn_in['wv'], 'L0_xattn_wo': _L0_xattn_in['wo'], 'L0_xattn_norm_w': _L0_xattn_in['norm_w'], 'L1_xattn_sa_wq': _L1_xattn_in['sa_wq'], 'L1_xattn_sa_bq': _L1_xattn_in['sa_bq'], 'L1_xattn_sa_wk': _L1_xattn_in['sa_wk'], 'L1_xattn_sa_bk': _L1_xattn_in['sa_bk'], 'L1_xattn_sa_wv': _L1_xattn_in['sa_wv'], 'L1_xattn_sa_bv': _L1_xattn_in['sa_bv'], 'L1_xattn_sa_wo': _L1_xattn_in['sa_wo'], 'L1_xattn_sa_bo': _L1_xattn_in['sa_bo'], 'L1_xattn_ca_wq': _L1_xattn_in['ca_wq'], 'L1_xattn_ca_bq': _L1_xattn_in['ca_bq'], 'L1_xattn_ca_wk': _L1_xattn_in['ca_wk'], 'L1_xattn_ca_bk': _L1_xattn_in['ca_bk'], 'L1_xattn_ca_wv': _L1_xattn_in['ca_wv'], 'L1_xattn_ca_bv': _L1_xattn_in['ca_bv'], 'L1_xattn_ca_wo': _L1_xattn_in['ca_wo'], 'L1_xattn_ca_bo': _L1_xattn_in['ca_bo'], 'L1_xattn_ln1_g': _L1_xattn_in['ln1_g'], 'L1_xattn_ln1_b': _L1_xattn_in['ln1_b'], 'L1_xattn_ln2_g': _L1_xattn_in['ln2_g'], 'L1_xattn_ln2_b': _L1_xattn_in['ln2_b'], 'L1_xattn_ln3_g': _L1_xattn_in['ln3_g'], 'L1_xattn_ln3_b': _L1_xattn_in['ln3_b'], 'L1_xattn_router_w': _L1_xattn_in['router_w'], 'L1_xattn_router_b': _L1_xattn_in['router_b'], 'L1_xattn_e_w1': _L1_xattn_in['e_w1'], 'L1_xattn_e_b1': _L1_xattn_in['e_b1'], 'L1_xattn_e_w2': _L1_xattn_in['e_w2'], 'L1_xattn_e_b2': _L1_xattn_in['e_b2']}

def reference(x, ctx_1024, L0_xattn_wq, L0_xattn_wk, L0_xattn_wv, L0_xattn_wo, L0_xattn_norm_w, L1_xattn_sa_wq, L1_xattn_sa_bq, L1_xattn_sa_wk, L1_xattn_sa_bk, L1_xattn_sa_wv, L1_xattn_sa_bv, L1_xattn_sa_wo, L1_xattn_sa_bo, L1_xattn_ca_wq, L1_xattn_ca_bq, L1_xattn_ca_wk, L1_xattn_ca_bk, L1_xattn_ca_wv, L1_xattn_ca_bv, L1_xattn_ca_wo, L1_xattn_ca_bo, L1_xattn_ln1_g, L1_xattn_ln1_b, L1_xattn_ln2_g, L1_xattn_ln2_b, L1_xattn_ln3_g, L1_xattn_ln3_b, L1_xattn_router_w, L1_xattn_router_b, L1_xattn_e_w1, L1_xattn_e_b1, L1_xattn_e_w2, L1_xattn_e_b2):
    import jax
    import jax.numpy as jnp

    def _L0_xattn_ref(hidden_states, key_value_states, wq, wk, wv, wo, norm_w):
        import jax, jax.numpy as jnp
        import numpy as np
        B, Q, KV = (2, 256, 256)
        D_MODEL = 128
        N_HEADS = 16
        D_KV = 64
        EPS = 1e-06
        var = jnp.mean(jnp.square(hidden_states), axis=-1, keepdims=True)
        normed = hidden_states * jax.lax.rsqrt(var + EPS) * norm_w
        b, q_len, _ = hidden_states.shape
        kv_len = key_value_states.shape[1]

        def split_heads(x):
            return x.reshape(b, -1, N_HEADS, D_KV).transpose(0, 2, 1, 3)
        q = split_heads(normed @ wq)
        k = split_heads(key_value_states @ wk)
        v = split_heads(key_value_states @ wv)
        scores = jnp.einsum('bhqd,bhkd->bhqk', q, k)
        attn = jax.nn.softmax(scores.astype(jnp.float32), axis=-1).astype(scores.dtype)
        ctx = jnp.einsum('bhqk,bhkd->bhqd', attn, v)
        ctx = ctx.transpose(0, 2, 1, 3).reshape(b, q_len, N_HEADS * D_KV)
        attn_out = ctx @ wo
        return hidden_states + attn_out

    def _L1_xattn_ref(x, encoder_output, sa_wq, sa_bq, sa_wk, sa_bk, sa_wv, sa_bv, sa_wo, sa_bo, ca_wq, ca_bq, ca_wk, ca_bk, ca_wv, ca_bv, ca_wo, ca_bo, ln1_g, ln1_b, ln2_g, ln2_b, ln3_g, ln3_b, router_w, router_b, e_w1, e_b1, e_w2, e_b2):
        import jax, jax.numpy as jnp
        import numpy as np
        B, S, SE, D, H, FF, E, K = (2, 256, 256, 128, 16, 512, 8, 2)
        HD = D // H

        def _layernorm(x, g, b):
            m = x.mean(-1, keepdims=True)
            v = ((x - m) ** 2).mean(-1, keepdims=True)
            return (x - m) / jnp.sqrt(v + 1e-05) * g + b

        def _attn(q_in, k_in, v_in, wq, bq, wk, bk, wv, bv, wo, bo, causal):
            Bq, Sq, Dm = q_in.shape
            Sk = k_in.shape[1]
            Q = (q_in @ wq + bq).reshape(Bq, Sq, H, HD)
            Kp = (k_in @ wk + bk).reshape(Bq, Sk, H, HD)
            V = (v_in @ wv + bv).reshape(Bq, Sk, H, HD)
            scores = jnp.einsum('bqhd,bkhd->bhqk', Q, Kp) / jnp.sqrt(jnp.float32(HD))
            if causal:
                mask = jnp.tril(jnp.ones((Sq, Sk), bool))
                scores = jnp.where(mask, scores, -jnp.inf)
            a = jax.nn.softmax(scores, axis=-1)
            o = jnp.einsum('bhqk,bkhd->bqhd', a, V).reshape(Bq, Sq, Dm)
            return o @ wo + bo

        def _moe(x, rw, rb, w1, b1, w2, b2):
            T = x.shape[0] * x.shape[1]
            xf = x.reshape(T, D)
            router_weights = jax.nn.softmax(xf @ rw + rb, axis=-1)
            topw, topi = jax.lax.top_k(router_weights, K)
            topw = jax.nn.softmax(topw, axis=-1)
            combine = jnp.zeros((T, E), xf.dtype).at[jnp.arange(T)[:, None], topi].add(topw)
            h = jax.nn.gelu(jnp.einsum('td,edf->etf', xf, w1) + b1[:, None, :], approximate=False)
            eo = jnp.einsum('etf,efd->etd', h, w2) + b2[:, None, :]
            out = jnp.einsum('etd,te->td', eo, combine)
            return out.reshape(x.shape)
        x = _layernorm(x + _attn(x, x, x, sa_wq, sa_bq, sa_wk, sa_bk, sa_wv, sa_bv, sa_wo, sa_bo, True), ln1_g, ln1_b)
        x = _layernorm(x + _attn(x, encoder_output, encoder_output, ca_wq, ca_bq, ca_wk, ca_bk, ca_wv, ca_bv, ca_wo, ca_bo, False), ln2_g, ln2_b)
        x = _layernorm(x + _moe(x, router_w, router_b, e_w1, e_b1, e_w2, e_b2), ln3_g, ln3_b)
        return x
    x = _L0_xattn_ref(x, ctx_1024, L0_xattn_wq, L0_xattn_wk, L0_xattn_wv, L0_xattn_wo, L0_xattn_norm_w)
    x = _L1_xattn_ref(x, ctx_1024, L1_xattn_sa_wq, L1_xattn_sa_bq, L1_xattn_sa_wk, L1_xattn_sa_bk, L1_xattn_sa_wv, L1_xattn_sa_bv, L1_xattn_sa_wo, L1_xattn_sa_bo, L1_xattn_ca_wq, L1_xattn_ca_bq, L1_xattn_ca_wk, L1_xattn_ca_bk, L1_xattn_ca_wv, L1_xattn_ca_bv, L1_xattn_ca_wo, L1_xattn_ca_bo, L1_xattn_ln1_g, L1_xattn_ln1_b, L1_xattn_ln2_g, L1_xattn_ln2_b, L1_xattn_ln3_g, L1_xattn_ln3_b, L1_xattn_router_w, L1_xattn_router_b, L1_xattn_e_w1, L1_xattn_e_b1, L1_xattn_e_w2, L1_xattn_e_b2)
    return x

_drawn_inputs = setup_inputs


def setup_inputs(seed=0):
    import zlib

    import numpy as np

    out = dict(_drawn_inputs(seed))
    spreads = {'L0_xattn_norm_w': (1.0, 0.6),
     'L1_xattn_sa_bq': (0.0, 0.8),
     'L1_xattn_sa_bk': (0.0, 2.0),
     'L1_xattn_sa_bv': (0.0, 0.386),
     'L1_xattn_sa_bo': (0.0, 0.1),
     'L1_xattn_ca_bq': (0.0, 2.0),
     'L1_xattn_ca_bk': (0.0, 2.0),
     'L1_xattn_ca_bv': (0.0, 0.299),
     'L1_xattn_ca_bo': (0.0, 0.1),
     'L1_xattn_ln1_g': (1.0, 0.2),
     'L1_xattn_ln1_b': (0.0, 0.1),
     'L1_xattn_ln2_g': (1.0, 0.2),
     'L1_xattn_ln2_b': (0.0, 0.1),
     'L1_xattn_ln3_g': (1.0, 0.2),
     'L1_xattn_ln3_b': (0.0, 0.1),
     'L1_xattn_router_b': (0.0, 0.1),
     'L1_xattn_e_b1': (0.0, 0.511),
     'L1_xattn_e_b2': (0.0, 0.1)}
    factors = {'L0_xattn_wq': 3.787,
     'L0_xattn_wk': 3.8,
     'L1_xattn_sa_wq': 8.0,
     'L1_xattn_sa_wk': 8.0,
     'L1_xattn_sa_wv': 5.238,
     'L1_xattn_ca_wq': 8.0,
     'L1_xattn_ca_wk': 8.0}
    for name, (base, spread) in spreads.items():
        noise = np.random.default_rng([zlib.crc32(name.encode()), seed]).standard_normal(out[name].shape)
        drawn = base * np.exp(spread * noise) if base else spread * noise
        out[name] = jnp.asarray(drawn.astype(out[name].dtype))
    for name, factor in factors.items():
        out[name] = (out[name] * factor).astype(out[name].dtype)
    return out
```

```python
from contextlib import ExitStack

import numpy as np
import concourse.bass as bass
from concourse import mybir

F32 = mybir.dt.float32
BF16 = mybir.dt.bfloat16
U32 = mybir.dt.uint32
ALU = mybir.AluOpType
ACT = mybir.ActivationFunctionType
AX = mybir.AxisListType

P = 128
B, S, D = 8, 256, 128
SC = 64
H, DK, HD = 16, 64, 8
E, FF = 8, 512
FC = FF // P
NP = H // 2
G = 4
GB = B // G
GT = GB * S // P
T = GB * S
CG = GB * SC
SLOTS = 6
Q_PART = [0, 0, 1, 1, 0, 2]
K_PART = [0, 1, 0, 1, 2, 0]
KR = SLOTS * 2 * HD
KM = KR + 4
NEG = -1.0e30
RMS_EPS, LN_EPS = 1e-6, 1e-5
SCALE = float(HD) ** -0.5

BIG = {"SETUP": 0, "KV": 0, "L0": 8, "SAP": 0, "SAM": 12, "SAE": 16, "SAO": 2,
       "CAP": 0, "CAM": 4, "CAE": 4, "CAO": 1, "R": 0, "MOE": 16}
SMALL = {"SETUP": 8, "KV": 8, "L0": 5, "SAP": 4, "SAM": 1, "SAE": 8, "SAO": 2,
         "CAP": 4, "CAM": 1, "CAE": 4, "CAO": 2, "R": 4, "MOE": 8}


def stage_order():
    order = [("SETUP", 0), ("KV", 0), ("L0", 0), ("KV", 1)]
    for g in range(G + 1):
        steps = [("SAP", g), ("CAP", g - 1), ("L0", g + 1), ("SAM", g), ("CAM", g - 1), ("KV", g + 2),
                 ("SAE", g), ("CAE", g - 1), ("SAO", g), ("CAO", g - 1), ("R", g - 1)]
        order += [(k, n) for k, n in steps if 0 <= n < G]
    return order + [("MOE", g) for g in range(G)]


ORDER = stage_order()


def first_jobs(count):
    at, out = 0, {}
    for kind, g in ORDER:
        out[kind, g] = at
        at += count[kind]
    return out


BIG0, SMALL0 = first_jobs(BIG), first_jobs(SMALL)
L0_BIG = {("S", 0): 0, ("S", 1): 1, ("T", 0): 2, ("S", 2): 3, ("T", 1): 4, ("S", 3): 5, ("T", 2): 6, ("T", 3): 7}


def xattn_layer_kernel(nc, x, ctx_t, wq_t, wk_t, wv_t, wo, norm_w, sa_w, ca_w, bqk, rows, router_w,
                       w1, b1, w2, b2, out):
    with ExitStack() as stack:
        def sb(name, shape, dt=F32):
            return stack.enter_context(nc.sbuf_tensor(name, shape, dt))

        def sem(name):
            return stack.enter_context(nc.semaphore(name))

        xs = sb("xs", [P, G * GT, D])
        ctxT = sb("ctxT", [P, B * SC])
        fold_w = sb("fold_w", [P, 4, NP, P])
        w1_sb = fold_w[:, :, :, :].rearrange("p a j n -> p (a j n)").rearrange("p (e f) -> p e f", e=E)
        mF = sb("mF", [P, 2, NP, P])
        nF = sb("nF", [P, 2, NP, P])
        normw = sb("normw", [P, 1])
        kf = sb("kf", [P, 2, GB * H * SC])
        vf = sb("vf", [P, 2, GB * NP * P])
        w2_sb = kf[:, :, :].rearrange("p a n -> p (a n)").rearrange("p (e c n) -> p e c n", e=E, c=FC)
        xn = sb("xn", [P, GT, D])
        xnT = sb("xnT", [P, T])
        prs = sb("prs", [P, 4, H * SC])
        pr, prT = prs[:, 0:2, :], prs[:, 2:4, :]
        hid = prs[:, :, :].rearrange("p a n -> p (a n)").rearrange("p (a c t) -> p a c t", a=2, c=FC)
        x1T = sb("x1T", [P, T])
        split32 = sb("split32", [P, T])
        parts = sb("parts", [P, 2, 3, T], BF16)
        qs = sb("qs", [P, NP, T], BF16)
        ks = sb("ks", [P, NP, 2, T], BF16)
        qc = sb("qc", [P, NP, T], BF16)
        kc = sb("kc", [P, NP, GB, 2 * SC], BF16)
        negm = sb("negm", [P, GT, H])
        mparts = sb("mparts", [H, 2, T], BF16)
        vaug = sb("vaug", [P, GT, H, 32])
        vblk = sb("vblk", [P, GB, NP, 32])
        pt = sb("pt", [P, 4, 2, 384])
        ptc = pt[:, :, :, :].rearrange("p a b n -> p (a b n)")[:, 0:2048].rearrange(
            "p (a j q) -> p a j q", a=2, j=4)
        oT = sb("oT", [P, GB, 4, S])
        oTc = sb("oTc", [P, GB, 2, S])
        rsum = sb("rsum", [P, GT * H])
        o_sb = sb("o_sb", [P, GT, D])
        oTn = sb("oTn", [P, T])
        sa_sb = sb("sa_sb", [P, 4, D])
        ca_sb = sb("ca_sb", [P, 4, D])
        bqk_sb = sb("bqk_sb", [P, 4])
        rows_sb = sb("rows_sb", [P, 10 * D + 2 * E])
        bc = rows_sb[:, 0:4 * D].rearrange("p (a d) -> p a d", a=4)
        lnr = rows_sb[:, 4 * D:10 * D].rearrange("p (a d) -> p a d", a=6)
        rb_sb = rows_sb[:, 10 * D:10 * D + E]
        iota = rows_sb[:, 10 * D + E:10 * D + 2 * E]
        rw_sb = sb("rw_sb", [P, E])
        b1_sb = sb("b1_sb", [P, E * FC])
        b2_sb = sb("b2_sb", [E, D])
        x3T = sb("x3T", [P, G * T])
        comb = sb("comb", [P, G * GT, E])
        combT = sb("combT", [E, T])
        ident = sb("ident", [P, P])
        identb = sb("identb", [P, P], BF16)
        mask_q = sb("mask_q", [P, P], BF16)
        mask_k = sb("mask_k", [P, P], BF16)
        mhalf = sb("mhalf", [P, 1])
        st = sb("st", [P, GT, 6])
        var = sb("var", [P, GT])
        mv = sb("mv", [P, GT, 2])
        rstd = sb("rstd", [P, GT])
        l0m = sb("l0m", [P, 2, H])
        l0s = sb("l0s", [P, 2, H])
        rt = sb("rt", [P, 6, GT, E])
        rs = sb("rs", [P, 8, GT])
        idx = sb("idx", [P, GT, E], U32)

        big = [stack.enter_context(nc.psum_tensor(f"big{i}", [P, 1024], F32)) for i in range(3)]
        small = [stack.enter_context(nc.psum_tensor(f"small{i}", [P, 512], F32)) for i in range(2)]

        parts_d = nc.dram_tensor("parts_d", [2, G, 2, P, 3, T], BF16, kind="Internal").ap()
        m_d = nc.dram_tensor("m_d", [2, G, H, 2, T], BF16, kind="Internal").ap()

        big_full = [sem(f"big_full{i}") for i in range(3)]
        big_free = [sem(f"big_free{i}") for i in range(3)]
        small_full = [sem(f"small_full{i}") for i in range(2)]
        small_free = [sem(f"small_free{i}") for i in range(2)]
        ld_x, ld_ctx, ld_fold, ld_layer = sem("ld_x"), sem("ld_ctx"), sem("ld_fold"), sem("ld_layer")
        ld_w1, ld_w2 = sem("ld_w1"), sem("ld_w2")
        consts_ready = sem("consts_ready")
        zeros_ready = sem("zeros_ready")
        ones_ready = sem("ones_ready")
        dve_step = sem("dve_step")
        pool_step = sem("pool_step")
        var_ready = sem("var_ready")
        rstd_ready = sem("rstd_ready")
        xn_ready = sem("xn_ready")
        exp_ready = sem("exp_ready")
        rec_ready = sem("rec_ready")
        probs_ready = sem("probs_ready")
        parts_ready = sem("parts_ready")
        parts_stored = sem("parts_stored")
        stack_s, stack_c = sem("stack_s"), sem("stack_c")
        m_stored = sem("m_stored")
        m_s, m_c = sem("m_s"), sem("m_c")
        ln_ready = sem("ln_ready")
        logit_ready = sem("logit_ready")
        rexp_ready = sem("rexp_ready")
        comb_ready = sem("comb_ready")
        res_ready = sem("res_ready")
        out_done = sem("out_done")

        def wait_big_full(eng, n):
            eng.wait_ge(big_full[n % 3], n // 3 + 1)

        def wait_big_free(eng, n):
            if n >= 0:
                eng.wait_ge(big_free[n % 3], n // 3 + 1)

        def wait_small_full(eng, n):
            eng.wait_ge(small_full[n % 2], n // 2 + 1)

        def wait_small_free(eng, n):
            if n >= 0:
                eng.wait_ge(small_free[n % 2], n // 2 + 1)

        STACK_S = 16 * (SLOTS + 2 * SLOTS)
        STACK_C = 16 * (SLOTS + 2 * GB * SLOTS)

        def turn(*kinds):
            return {kg: i for i, kg in enumerate(kg for kg in ORDER if kg[0] in kinds)}

        proj_turn, max_turn = turn("SAP", "CAP"), turn("SAM", "CAM")
        norm_turn, var_turn = turn("SAO", "CAO"), turn("L0", "SAO", "CAO", "MOE")

        block = stack.enter_context(nc.Block())

        @block.sync
        def _(sp):
            sp.dma_start(ctxT[:, :], ctx_t).then_inc(ld_ctx, 16)
            sp.dma_start(fold_w[:, 0], wq_t.rearrange("(j p) n -> p j n", p=P)).then_inc(ld_fold, 16)
            sp.dma_start(fold_w[:, 2], wv_t.rearrange("(j p) n -> p j n", p=P)).then_inc(ld_fold, 16)
            sp.dma_start(normw[:, :], norm_w).then_inc(ld_fold, 16)
            sp.dma_start(sa_sb[:, :, :], sa_w.rearrange("a d n -> d a n")).then_inc(ld_layer, 16)
            sp.dma_start(bqk_sb[:, :], bqk).then_inc(ld_layer, 16)
            sp.dma_start(rows_sb[:, :], rows.broadcast_to([P, 10 * D + 2 * E])).then_inc(ld_layer, 16)
            sp.dma_start(ca_sb[:, :, :], ca_w.rearrange("a d n -> d a n")).then_inc(ld_layer, 16)
            sp.dma_start(rw_sb[:, :], router_w).then_inc(ld_layer, 16)
            sp.dma_start(b1_sb[:, :], b1).then_inc(ld_layer, 16)
            sp.dma_start(b2_sb[:, :], b2).then_inc(ld_layer, 16)
            wait_small_full(sp, SMALL0["SETUP", 0] + 6)
            wait_small_full(sp, SMALL0["SETUP", 0] + 7)
            sp.dma_start(w1_sb, w1.rearrange("e d f -> d e f")).then_inc(ld_w1, 16)

            def parts_and_stacks(kind, g):
                a = 0 if kind == "SAP" else 1
                turns, wide = proj_turn[kind, g], T if kind == "SAP" else CG
                for which, n in ((0, T), (1, wide)):
                    sp.wait_ge(parts_ready, 2 * turns + which + 1)
                    sp.dma_start(parts_d[a, g, which, :, :, 0:n], parts[:, which, :, 0:n]).then_inc(parts_stored, 16)
                if g > 0 and a == 0:
                    wait_big_full(sp, BIG0["SAE", g - 1] + BIG["SAE"] - 1)
                if g > 0 and a == 1:
                    wait_big_full(sp, BIG0["CAE", g - 1] + BIG["CAE"] - 1)
                ready = stack_c if a else stack_s
                sp.wait_ge(parts_stored, 32 * turns + 32)
                for s in range(SLOTS):
                    src = parts_d[a, g, 0, :, Q_PART[s], :].rearrange("(j r) t -> r j t", j=NP)
                    sp.dma_start((qc if a else qs)[2 * HD * s:2 * HD * (s + 1), :, :], src).then_inc(ready, 16)
                for s in range(SLOTS):
                    for h2 in range(2):
                        r = 2 * HD * s + HD * h2
                        src = parts_d[a, g, 1, :, K_PART[s], 0:wide].rearrange("(j h d) t -> h d j t", j=NP, h=2)[h2]
                        if a == 0:
                            sp.dma_start(ks[r:r + HD, :, h2, :], src).then_inc(ready, 16)
                        else:
                            for b in range(GB):
                                sp.dma_start(kc[r:r + HD, :, b, h2 * SC:(h2 + 1) * SC],
                                             src[:, :, b * SC:(b + 1) * SC]).then_inc(ready, 16)

            def maxima(kind, g):
                a = 0 if kind == "SAM" else 1
                wait_small_free(sp, SMALL0[kind, g])
                sp.dma_start(m_d[a, g], mparts[:, :, :]).then_inc(m_stored, 16)
                sp.wait_ge(m_stored, 16 * max_turn[kind, g] + 16)
                for part in range(2):
                    src = m_d[a, g, :, part, :].rearrange("(j h) t -> h j t", j=NP)
                    sp.dma_start((qc if a else qs)[KR + 2 * part:KR + 2 * part + 2, :, :], src).then_inc(
                        m_c if a else m_s, 16)

            for kind, g in ORDER:
                if kind in ("SAP", "CAP"):
                    parts_and_stacks(kind, g)
                if kind in ("SAM", "CAM"):
                    maxima(kind, g)
                if (kind, g) == ("L0", G - 1):
                    wait_big_full(sp, BIG0[kind, g] + L0_BIG["S", GT - 1])
                    sp.dma_start(w2_sb, w2.rearrange("e (c p) n -> p e c n", p=P)).then_inc(ld_w2, 16)
                if kind == "MOE":
                    sp.wait_ge(res_ready, g + 1)
                    sp.dma_start(out.rearrange("(t p) d -> p t d", p=P)[:, g * GT:(g + 1) * GT],
                                 xs[:, g * GT:(g + 1) * GT, :]).then_inc(out_done, 16)
            sp.wait_ge(out_done, 16 * G)

        @block.gpsimd
        def _(pool):
            steps = [0]

            def step(ins):
                steps[0] += 1
                ins.then_inc(pool_step, 1)
                pool.wait_ge(pool_step, steps[0])

            step(nc.gpsimd.memset(ident[:, :], 0.0))
            nc.gpsimd.affine_select(out=ident[:, :], in_=ident[:, :], compare_op=ALU.not_equal, fill=1.0, base=0,
                                    pattern=[[-1, P]], channel_multiplier=1).then_inc(consts_ready, 1)
            step(nc.gpsimd.memset(identb[:, :], 0.0))
            nc.gpsimd.affine_select(out=identb[:, :], in_=identb[:, :], compare_op=ALU.not_equal, fill=1.0, base=0,
                                    pattern=[[-1, P]], channel_multiplier=1).then_inc(consts_ready, 1)
            step(nc.gpsimd.memset(mask_q[:, :], 0.0))
            nc.gpsimd.affine_select(out=mask_q[:, :], in_=mask_q[:, :], compare_op=ALU.is_ge, fill=NEG, base=0,
                                    pattern=[[-1, P]], channel_multiplier=1).then_inc(consts_ready, 1)
            step(nc.gpsimd.memset(mask_k[:, :], 0.0))
            nc.gpsimd.affine_select(out=mask_k[:, :], in_=mask_k[:, :], compare_op=ALU.is_ge, fill=NEG, base=0,
                                    pattern=[[1, P]], channel_multiplier=-1).then_inc(consts_ready, 1)

            def ones_rows(rows4, pattern):
                for base in (0, -2):
                    ins = nc.gpsimd.affine_select(out=rows4, in_=rows4, compare_op=ALU.not_equal, fill=1.0,
                                                  base=base, pattern=pattern, channel_multiplier=1)
                    if base == 0:
                        step(ins)
                ins.then_inc(ones_ready, 1)

            def power(kind, g):
                pool.wait_ge(var_ready, var_turn[kind, g] + 1)
                nc.gpsimd.tensor_tensor(rstd[:, :], var[:, :], mhalf[:, :].broadcast_to([P, GT]),
                                        ALU.pow).then_inc(rstd_ready, 1)

            for kind, g in ORDER:
                if kind == "L0":
                    power(kind, g)
                    for t in range(GT):
                        pool.wait_ge(rec_ready, GT * g + t + 1)
                        pv = pr[:, t % 2, :].rearrange("p (h k) -> p h k", h=H)
                        nc.gpsimd.tensor_tensor(pv, pv, l0s[:, t % 2, :].unsqueeze(2).broadcast_to([P, H, SC]),
                                                ALU.mult).then_inc(probs_ready, 1)
                    if g == 0:
                        pool.wait_ge(zeros_ready, 1)
                        pool.wait_ge(probs_ready, GT)
                        ones_rows(ks[KR:KM, :, :, :], [[0, NP], [-1, 2], [0, T]])
                        pool.wait_ge(ones_ready, 1)
                        ones_rows(kc[KR:KM, :, :, :].rearrange("p j b (h k) -> p (j b) h k", h=2),
                                  [[0, NP * GB], [-1, 2], [0, SC]])
                        pool.wait_ge(ones_ready, 2)
                if kind in ("SAO", "CAO", "MOE"):
                    power(kind, g)

        @block.scalar
        def _(act):
            act.dma_start(xs[:, :, :], x.rearrange("(t p) d -> p t d", p=P)).then_inc(ld_x, 16)
            act.dma_start(fold_w[:, 1], wk_t.rearrange("(j p) n -> p j n", p=P)).then_inc(ld_fold, 16)
            act.dma_start(fold_w[:, 3], wo.rearrange("(j p) n -> p j n", p=P)).then_inc(ld_fold, 16)

            def copy_small(n, dst, width=512):
                wait_small_full(act, n)
                nc.scalar.copy(dst, small[n % 2][:, 0:width]).then_inc(small_free[n % 2], 1)

            def setup(g):
                for i in range(4):
                    n = SMALL0["SETUP", 0] + i
                    copy_small(n, mF[:, i % 2, 4 * (i // 2):4 * (i // 2) + 4, :])

            def kv(g):
                if g == 0:
                    act.wait_ge(ld_fold, 16 * 5)
                for i in range(4):
                    n = SMALL0["KV", g] + 2 * i
                    wait_small_full(act, n)
                    dst = kf[:, g % 2, :].rearrange("p (b j h k) -> p h j b k", b=GB, j=NP, h=2)
                    for b in range(GB):
                        ins = nc.scalar.activation(
                            dst[:, i % 2, 4 * (i // 2):4 * (i // 2) + 4, b],
                            small[n % 2][:, :].rearrange("p (j b k) -> p j b k", j=4, b=GB)[:, :, b],
                            ACT.Copy, scale=normw[:, 0:1])
                    ins.then_inc(small_free[n % 2], 1)

            def first_attention(g):
                s0, b0 = SMALL0["L0", g], BIG0["L0", g]
                copy_small(s0, xnT[:, :])

                def exp(t):
                    wait_big_free(act, b0 + L0_BIG["S", t])
                    nc.scalar.activation(pr[:, t % 2, :], pr[:, t % 2, :], ACT.Exp).then_inc(exp_ready, 1)

                def transposed(t):
                    n = b0 + L0_BIG["T", t]
                    wait_big_full(act, n)
                    nc.scalar.copy(prT[:, t % 2, :], big[n % 3][:, :]).then_inc(big_free[n % 3], 1)

                exp(0)
                exp(1)
                transposed(0)
                exp(2)
                transposed(1)
                exp(3)
                transposed(2)
                transposed(3)

            def self_exp(g):
                for p in range(GB * NP):
                    n = BIG0["SAE", g] + p
                    wait_big_full(act, n)
                    nc.scalar.activation(pt[:, p % 4, :, :],
                                         big[n % 3][:, :].rearrange("p (h n) -> p h n", h=2)[:, :, 0:384],
                                         ACT.Exp).then_inc(big_free[n % 3], 1)

            def cross_exp(g):
                for i in range(2 * GB):
                    n = BIG0["CAE", g] + i
                    wait_big_full(act, n)
                    nc.scalar.activation(ptc[:, i % 2], big[n % 3][:, :].rearrange("p (j q) -> p j q", j=4),
                                         ACT.Exp).then_inc(big_free[n % 3], 1)

            def router(g):
                copy_small(SMALL0["R", g], x3T[:, g * T:(g + 1) * T])
                act.wait_ge(logit_ready, 2 * g + 1)
                nc.scalar.activation(rt[:, 1, :, :], rt[:, 0, :, :], ACT.Exp).then_inc(rexp_ready, 1)
                act.wait_ge(logit_ready, 2 * g + 2)
                nc.scalar.activation(rs[:, 3, :], rs[:, 2, :], ACT.Exp).then_inc(rexp_ready, 1)

            def experts(g):
                for e in range(E):
                    for c in range(FC):
                        n = BIG0["MOE", g] + 2 * e + c // 2
                        if c % 2 == 0:
                            wait_big_full(act, n)
                        ins = nc.scalar.activation(hid[:, e % 2, c, :], big[n % 3][:, (c % 2) * T:(c % 2 + 1) * T],
                                                   ACT.Gelu, bias=b1_sb[:, e * FC + c:e * FC + c + 1])
                        if c % 2 == 1:
                            ins.then_inc(big_free[n % 3], 1)

            for kind, g in ORDER:
                if kind == "SETUP":
                    setup(g)
                if kind == "KV":
                    kv(g)
                if kind == "L0":
                    first_attention(g)
                if kind in ("SAP", "CAP"):
                    copy_small(SMALL0[kind, g], x1T[:, :])
                if kind == "SAE":
                    self_exp(g)
                if kind == "CAE":
                    cross_exp(g)
                if kind in ("SAO", "CAO"):
                    copy_small(SMALL0[kind, g], oTn[:, :])
                if kind == "R":
                    router(g)
                if kind == "MOE":
                    if g == 0:
                        act.wait_ge(ld_layer, 16 * 7)
                    experts(g)

        @block.vector
        def _(dve):
            steps = [0]

            def step(ins):
                steps[0] += 1
                ins.then_inc(dve_step, 1)
                dve.wait_ge(dve_step, steps[0])

            def setup(g):
                nc.vector.memset(mhalf[:, :], -0.5)
                nc.vector.memset(ks[:, :, :, :].bitcast(U32), 0)
                nc.vector.memset(kc[:, :, :, :].bitcast(U32), 0)
                nc.vector.memset(vaug[:, :, :, :], 0.0)
                step(nc.vector.memset(vblk[:, :, :, :], 0.0))
                nc.vector.memset(vaug[:, :, :, HD:HD + 1], 1.0)
                nc.vector.memset(vblk[0:SC, :, :, HD:HD + 1], 1.0)
                nc.vector.memset(vblk[SC:P, :, :, 16 + HD:16 + HD + 1], 1.0).then_inc(zeros_ready, 1)
                for i in range(4):
                    n = SMALL0["SETUP", 0] + 4 + i
                    wait_small_full(dve, n)
                    nc.vector.tensor_copy(nF[:, i % 2, 4 * (i // 2):4 * (i // 2) + 4, :],
                                          small[n % 2][:, :]).then_inc(small_free[n % 2], 1)

            def kv(g):
                for i in range(4):
                    n = SMALL0["KV", g] + 2 * i + 1
                    wait_small_full(dve, n)
                    nc.vector.tensor_copy(vf[:, g % 2, i * 512:(i + 1) * 512],
                                          small[n % 2][:, :]).then_inc(small_free[n % 2], 1)

            def group(g):
                return xs[:, g * GT:(g + 1) * GT, :]

            def wide(ap):
                return ap.unsqueeze(2).broadcast_to([P, GT, D])

            def first_attention(g):
                s0, b0 = SMALL0["L0", g], BIG0["L0", g]
                if g == 0:
                    dve.wait_ge(ld_x, 16)
                step(nc.vector.tensor_tensor(xn[:, :, :], group(g), group(g), ALU.mult))
                step(nc.vector.reduce_sum(var[:, :], xn[:, :, :], AX.X))
                nc.vector.tensor_scalar(var[:, :], var[:, :], 1.0 / D, RMS_EPS, ALU.mult, ALU.add).then_inc(var_ready, 1)
                dve.wait_ge(rstd_ready, var_turn["L0", g] + 1)
                nc.vector.tensor_tensor(xn[:, :, :], group(g), wide(rstd[:, :]), ALU.mult).then_inc(xn_ready, 1)

                def diff(t):
                    n = b0 + L0_BIG["S", t]
                    wait_big_full(dve, n)
                    scores = big[n % 3][:, :].rearrange("p (h k) -> p h k", h=H)
                    step(nc.vector.reduce_max(l0m[:, t % 2, :], scores, AX.X, negate=True))
                    nc.vector.tensor_tensor(pr[:, t % 2, :].rearrange("p (h k) -> p h k", h=H), scores,
                                            l0m[:, t % 2, :].unsqueeze(2).broadcast_to([P, H, SC]),
                                            ALU.add).then_inc(big_free[n % 3], 1)

                def sums(t):
                    dve.wait_ge(exp_ready, GT * g + t + 1)
                    step(nc.vector.reduce_sum(l0s[:, t % 2, :], pr[:, t % 2, :].rearrange("p (h k) -> p h k", h=H), AX.X))
                    nc.vector.reciprocal(l0s[:, t % 2, :], l0s[:, t % 2, :]).then_inc(rec_ready, 1)

                def residual(t):
                    n = s0 + 1 + t
                    wait_small_full(dve, n)
                    nc.vector.tensor_tensor(xs[:, g * GT + t, :], xs[:, g * GT + t, :], small[n % 2][:, 0:D],
                                            ALU.add).then_inc(small_free[n % 2], 1)

                diff(0)
                diff(1)
                sums(0)
                diff(2)
                sums(1)
                residual(0)
                diff(3)
                sums(2)
                residual(1)
                sums(3)
                residual(2)
                residual(3)

            def split(n, width, bias, scale, turns, which):
                q = split32[:, 0:width]
                part = [parts[:, which, i, 0:width] for i in range(3)]
                wait_small_full(dve, n)
                nc.vector.tensor_scalar(q, small[n % 2][:, 0:width], bias, scale, ALU.add,
                                        ALU.mult).then_inc(small_free[n % 2], 1)
                wait_small_free(dve, n)
                if turns > 0:
                    dve.wait_ge(parts_stored, 32 * turns)
                step(nc.vector.tensor_copy(part[0], q))
                step(nc.vector.tensor_tensor(q, q, part[0], ALU.subtract))
                step(nc.vector.tensor_copy(part[1], q))
                nc.vector.tensor_tensor(part[2], q, part[1], ALU.subtract).then_inc(parts_ready, 1)
                dve.wait_ge(parts_ready, 2 * turns + which + 1)

            def self_projections(g):
                n, turns = SMALL0["SAP", g], proj_turn["SAP", g]
                if g == 0:
                    dve.wait_ge(ld_layer, 16 * 7)
                split(n + 1, T, bqk_sb[:, 0:1], SCALE, turns, 0)
                split(n + 2, T, bqk_sb[:, 1:2], 1.0, turns, 1)
                n += 3
                wait_small_full(dve, n)
                for t in range(GT):
                    ins = nc.vector.tensor_tensor(vaug[:, t, :, 0:HD],
                                                  small[n % 2][:, t * D:(t + 1) * D].rearrange("p (h d) -> p h d", h=H),
                                                  bc[:, 0, :].rearrange("p (h d) -> p h d", h=H), ALU.add)
                ins.then_inc(small_free[n % 2], 1)

            def cross_projections(g):
                n, turns = SMALL0["CAP", g], proj_turn["CAP", g]
                split(n + 1, T, bqk_sb[:, 2:3], SCALE, turns, 0)
                split(n + 2, CG, bqk_sb[:, 3:4], 1.0, turns, 1)
                n += 3
                wait_small_full(dve, n)
                for h2 in range(2):
                    half = slice(h2 * SC, (h2 + 1) * SC)
                    for b in range(GB):
                        ins = nc.vector.tensor_tensor(
                            vblk[half, b, :, 16 * h2:16 * h2 + HD],
                            small[n % 2][half, b * 64:(b + 1) * 64].rearrange("p (j d) -> p j d", j=NP),
                            bc[half, 2, :].rearrange("p (j h d) -> p h j d", j=NP, h=2)[:, h2], ALU.add)
                ins.then_inc(small_free[n % 2], 1)

            def max_parts(kind, g):
                n = SMALL0[kind, g]
                wait_small_full(dve, n)
                if max_turn[kind, g] > 0:
                    dve.wait_ge(m_stored, 16 * max_turn[kind, g])
                step(nc.vector.tensor_copy(mparts[:, 0, :], small[n % 2][0:H, :]))
                nc.vector.tensor_tensor(mparts[:, 1, :], small[n % 2][0:H, :], mparts[:, 0, :],
                                        ALU.subtract).then_inc(small_free[n % 2], 1)

            def self_max(g):
                n = BIG0["SAM", g]
                for t in range(GT):
                    jobs, keys = (2, P) if t % 2 == 0 else (4, 2 * P)
                    heads = H // jobs
                    for a in range(jobs):
                        wait_big_full(dve, n)
                        nc.vector.reduce_max(negm[:, t, a * heads:(a + 1) * heads],
                                             big[n % 3][:, :].rearrange("p (h k) -> p h k", k=keys), AX.X,
                                             negate=True).then_inc(big_free[n % 3], 1)
                        n += 1
                max_parts("SAM", g)

            def cross_max(g):
                for t in range(GT):
                    n = BIG0["CAM", g] + t
                    wait_big_full(dve, n)
                    nc.vector.reduce_max(negm[:, t, :], big[n % 3][:, :].rearrange("p (h k) -> p h k", k=SC), AX.X,
                                         negate=True).then_inc(big_free[n % 3], 1)
                max_parts("CAM", g)

            def head_outputs(kind, g):
                for i in range(SMALL[kind]):
                    n = SMALL0[kind, g] + i
                    wait_small_full(dve, n)
                    dst = oT[:, i // 4, i % 4, :] if kind == "SAE" else oTc[:, i // 2, i % 2, :]
                    nc.vector.tensor_copy(dst, small[n % 2][:, 0:S]).then_inc(small_free[n % 2], 1)

            def layernorm(kind, g, which, done):
                for t in range(GT):
                    ins = nc.vector.bn_stats(st[:, t, :], xs[:, g * GT + t, :])
                step(ins)
                for t in range(GT):
                    ins = nc.vector.bn_aggr(mv[:, t, :], st[:, t, :])
                step(ins)
                nc.vector.tensor_scalar(var[:, :], mv[:, :, 1], LN_EPS, None, ALU.add).then_inc(var_ready, 1)
                dve.wait_ge(rstd_ready, var_turn[kind, g] + 1)
                for t in range(GT):
                    ins = nc.vector.tensor_scalar(xs[:, g * GT + t, :], xs[:, g * GT + t, :], mv[:, t, 0:1],
                                                  rstd[:, t:t + 1], ALU.subtract, ALU.mult)
                step(ins)
                gain, shift = (lnr[:, 2 * which + i, :].unsqueeze(1).broadcast_to([P, GT, D]) for i in range(2))
                step(nc.vector.tensor_tensor(group(g), group(g), gain, ALU.mult))
                nc.vector.tensor_tensor(group(g), group(g), shift, ALU.add).then_inc(done, 1)

            def output(kind, g):
                a, stride = (0, 32) if kind == "SAO" else (1, 16)
                heads = 1024 // stride
                for i in range(BIG[kind]):
                    n = BIG0[kind, g] + i
                    wait_big_full(dve, n)
                    o = big[n % 3][:, :].rearrange("p (h c) -> p h c", c=stride)
                    r = rsum[:, i * heads:(i + 1) * heads]
                    step(nc.vector.reciprocal(r, o[:, :, HD]))
                    nc.vector.tensor_tensor(
                        o_sb[:, :, :].rearrange("p t (h d) -> p (t h) d", h=H)[:, i * heads:(i + 1) * heads, :],
                        o[:, :, 0:HD], r.unsqueeze(2).broadcast_to([P, heads, HD]),
                        ALU.mult).then_inc(big_free[n % 3], 1)
                n = SMALL0[kind, g] + 1
                wait_small_full(dve, n)
                nc.vector.tensor_tensor(group(g), group(g), small[n % 2][:, :].rearrange("p (t d) -> p t d", t=GT),
                                        ALU.add).then_inc(small_free[n % 2], 1)
                wait_small_free(dve, n)
                step(nc.vector.tensor_tensor(group(g), group(g),
                                             bc[:, 2 * a + 1, :].unsqueeze(1).broadcast_to([P, GT, D]), ALU.add))
                layernorm(kind, g, a, ln_ready)

            def router(g):
                n = SMALL0["R", g] + 1
                logits, prob, eq1, eq2 = rt[:, 0], rt[:, 1], rt[:, 2], rt[:, 3]
                m8, idf = rt[:, 4], rt[:, 5]
                neg, inv, dif, e2, w1_, w2_ = (rs[:, i, :] for i in range(6))

                def col(ap):
                    return ap.unsqueeze(2).broadcast_to([P, GT, E])

                def row(ap):
                    return ap.unsqueeze(1).broadcast_to([P, GT, E])

                wait_small_full(dve, n)
                nc.vector.tensor_tensor(logits, small[n % 2][:, 0:GT * E].rearrange("p (t e) -> p t e", t=GT),
                                        row(rb_sb), ALU.add).then_inc(small_free[n % 2], 1)
                wait_small_free(dve, n)
                step(nc.vector.reduce_max(neg, logits, AX.X, negate=True))
                nc.vector.tensor_tensor(logits, logits, col(neg), ALU.add).then_inc(logit_ready, 1)
                dve.wait_ge(rexp_ready, 2 * g + 1)
                step(nc.vector.reduce_sum(inv, prob, AX.X))
                step(nc.vector.reciprocal(inv, inv))
                step(nc.vector.tensor_tensor(prob, prob, col(inv), ALU.mult))
                for t in range(GT):
                    ins = nc.vector.max(m8[:, t, :], prob[:, t, :])
                step(ins)
                for t in range(GT):
                    ins = nc.vector.max_index(idx[:, t, :], m8[:, t, :], prob[:, t, :])
                step(ins)
                step(nc.vector.tensor_copy(idf, idx[:, :, :]))
                nc.vector.tensor_tensor(dif, m8[:, :, 1], m8[:, :, 0], ALU.subtract).then_inc(logit_ready, 1)
                dve.wait_ge(rexp_ready, 2 * g + 2)
                step(nc.vector.tensor_scalar(w1_, e2, 1.0, None, ALU.add))
                step(nc.vector.reciprocal(w1_, w1_))
                nc.vector.tensor_tensor(eq1, row(iota), col(idf[:, :, 0]), ALU.is_equal)
                nc.vector.tensor_tensor(eq2, row(iota), col(idf[:, :, 1]), ALU.is_equal)
                step(nc.vector.tensor_tensor(w2_, e2, w1_, ALU.mult))
                nc.vector.tensor_tensor(eq1, eq1, col(w1_), ALU.mult)
                step(nc.vector.tensor_tensor(eq2, eq2, col(w2_), ALU.mult))
                nc.vector.tensor_tensor(comb[:, g * GT:(g + 1) * GT, :], eq1, eq2, ALU.add).then_inc(comb_ready, 1)
                wait_small_full(dve, n + 1)
                nc.vector.tensor_copy(combT[:, :], small[(n + 1) % 2][0:E, :]).then_inc(small_free[(n + 1) % 2], 1)
                wait_small_full(dve, n + 2)
                nc.vector.tensor_tensor(group(g), group(g), small[(n + 2) % 2][:, :].rearrange("p (t d) -> p t d", t=GT),
                                        ALU.add).then_inc(small_free[(n + 2) % 2], 1)

            def experts(g):
                for e in range(E):
                    n = SMALL0["MOE", g] + e
                    wait_small_full(dve, n)
                    if e > 0:
                        wait_small_free(dve, n - 1)
                    for t in range(GT):
                        ins = nc.vector.scalar_tensor_tensor(
                            xs[:, g * GT + t, :], small[n % 2][:, t * D:(t + 1) * D], comb[:, g * GT + t, e:e + 1],
                            xs[:, g * GT + t, :], ALU.mult, ALU.add)
                    ins.then_inc(small_free[n % 2], 1)
                wait_small_free(dve, n)
                layernorm("MOE", g, 2, res_ready)

            for kind, g in ORDER:
                {"SETUP": setup, "KV": kv, "L0": first_attention, "SAP": self_projections, "SAM": self_max,
                 "CAP": cross_projections, "CAM": cross_max, "R": router, "MOE": experts}.get(
                    kind, lambda g: None)(g)
                if kind in ("SAE", "CAE"):
                    head_outputs(kind, g)
                if kind in ("SAO", "CAO"):
                    output(kind, g)

        @block.tensor
        def _(pe):
            def mm(out_, lhsT, rhs, start=True, stop=True):
                return nc.tensor.matmul(out_, lhsT, rhs, start=start, stop=stop)

            def small_job(n):
                wait_small_free(pe, n - 2)
                return small[n % 2]

            def big_job(n):
                wait_big_free(pe, n - 3)
                return big[n % 3]

            def setup(g):
                pe.wait_ge(ld_fold, 16 * 5)
                for i in range(8):
                    n = SMALL0["SETUP", 0] + i
                    bank = small_job(n)
                    h2, j0 = i % 2, 4 * (i % 4 // 2)
                    a, b = (1, 0) if i < 4 else (2, 3)
                    half = slice(64 * h2, 64 * h2 + 64)
                    for jj in range(4):
                        ins = mm(bank[:, jj * P:(jj + 1) * P], fold_w[half, a, j0 + jj, :], fold_w[half, b, j0 + jj, :])
                    ins.then_inc(small_full[n % 2], 1)

            def kv(g):
                if g == 0:
                    pe.wait_ge(ld_ctx, 16)
                    wait_small_free(pe, SMALL0["SETUP", 0] + 3)
                    wait_small_free(pe, SMALL0["SETUP", 0] + 2)
                for i in range(4):
                    n = SMALL0["KV", g] + 2 * i
                    bank = small_job(n)
                    for jj in range(4):
                        ins = mm(bank[:, jj * P:(jj + 1) * P], mF[:, i % 2, 4 * (i // 2) + jj, :],
                                 ctxT[:, g * CG:(g + 1) * CG])
                    ins.then_inc(small_full[n % 2], 1)
                    n, b, j0 = n + 1, i // 2, 4 * (i % 2)
                    bank = small_job(n)
                    if g == 0 and i == 0:
                        wait_small_free(pe, SMALL0["SETUP", 0] + 7)
                        wait_small_free(pe, SMALL0["SETUP", 0] + 6)
                    for h2 in range(2):
                        ins = mm(bank[64 * h2:64 * h2 + 64, :],
                                 ctxT[:, (g * GB + b) * SC:(g * GB + b + 1) * SC],
                                 nF[:, h2, j0:j0 + 4, :])
                    ins.then_inc(small_full[n % 2], 1)

            def transposes(n, sources, rows=P):
                bank = small_job(n)
                for t, src in enumerate(sources):
                    ins = nc.tensor.transpose(bank[0:rows, t * P:(t + 1) * P], src, ident[:, :])
                ins.then_inc(small_full[n % 2], 1)

            def first_attention(g):
                s0, b0 = SMALL0["L0", g], BIG0["L0", g]
                if g == 0:
                    pe.wait_ge(consts_ready, 4)
                pe.wait_ge(xn_ready, g + 1)
                transposes(s0, [xn[:, t, :] for t in range(GT)])
                wait_small_free(pe, s0)
                wait_small_free(pe, SMALL0["KV", g] + 6)
                wait_small_free(pe, SMALL0["KV", g] + 7)

                def scores(t):
                    n = b0 + L0_BIG["S", t]
                    unit = big_job(n)
                    for i in range(2):
                        at = (t // 2) * H * SC + i * 512
                        ins = mm(unit[:, i * 512:(i + 1) * 512], xnT[:, t * P:(t + 1) * P], kf[:, g % 2, at:at + 512])
                    ins.then_inc(big_full[n % 3], 1)

                def transpose_probs(t):
                    n = b0 + L0_BIG["T", t]
                    unit = big_job(n)
                    pe.wait_ge(probs_ready, GT * g + t + 1)
                    for j in range(NP):
                        ins = nc.tensor.transpose(unit[:, j * P:(j + 1) * P], pr[:, t % 2, j * P:(j + 1) * P], ident[:, :])
                    ins.then_inc(big_full[n % 3], 1)

                def values(t):
                    n = s0 + 1 + t
                    bank = small_job(n)
                    wait_big_free(pe, b0 + L0_BIG["T", t])
                    for j in range(NP):
                        at = ((t // 2) * NP + j) * P
                        ins = mm(bank[:, 0:D], prT[:, t % 2, j * P:(j + 1) * P], vf[:, g % 2, at:at + P],
                                 start=(j == 0), stop=(j == NP - 1))
                    ins.then_inc(small_full[n % 2], 1)

                scores(0)
                scores(1)
                transpose_probs(0)
                scores(2)
                values(0)
                transpose_probs(1)
                scores(3)
                values(1)
                transpose_probs(2)
                values(2)
                transpose_probs(3)
                values(3)

            def self_projections(g):
                n = SMALL0["SAP", g]
                if g == 0:
                    pe.wait_ge(ld_layer, 16 * 7)
                wait_small_free(pe, SMALL0["L0", g] + 4)
                wait_small_free(pe, SMALL0["L0", g] + 3)
                transposes(n, [xs[:, g * GT + t, :] for t in range(GT)])
                wait_small_free(pe, n)
                for i in range(2):
                    bank = small_job(n + 1 + i)
                    mm(bank[:, :], sa_sb[:, i, :], x1T[:, :]).then_inc(small_full[(n + 1 + i) % 2], 1)
                bank = small_job(n + 3)
                for t in range(GT):
                    ins = mm(bank[:, t * D:(t + 1) * D], x1T[:, t * P:(t + 1) * P], sa_sb[:, 2, :])
                ins.then_inc(small_full[(n + 3) % 2], 1)

            def cross_projections(g):
                n = SMALL0["CAP", g]
                pe.wait_ge(ln_ready, norm_turn["SAO", g] + 1)
                transposes(n, [xs[:, g * GT + t, :] for t in range(GT)])
                wait_small_free(pe, n)
                bank = small_job(n + 1)
                mm(bank[:, :], ca_sb[:, 0, :], x1T[:, :]).then_inc(small_full[(n + 1) % 2], 1)
                bank = small_job(n + 2)
                mm(bank[:, 0:CG], ca_sb[:, 1, :], ctxT[:, g * CG:(g + 1) * CG]).then_inc(small_full[(n + 2) % 2], 1)
                bank = small_job(n + 3)
                for b in range(GB):
                    for h2 in range(2):
                        ins = mm(bank[64 * h2:64 * h2 + 64, b * 64:(b + 1) * 64],
                                 ctxT[:, (g * GB + b) * SC:(g * GB + b + 1) * SC],
                                 ca_sb[:, 2, :].rearrange("p (j h d) -> p h j d", j=NP, h=2)[:, h2])
                ins.then_inc(small_full[(n + 3) % 2], 1)

            def self_max(g):
                if g == 0:
                    pe.wait_ge(ones_ready, 2)
                pe.wait_ge(stack_s, STACK_S * (g + 1))
                n = BIG0["SAM", g]
                for t in range(GT):
                    b, tile = t // 2, t % 2
                    keys = P * (tile + 1)
                    for j in range(NP):
                        width = 2 * keys
                        pairs = 1024 // width
                        if j % pairs == 0:
                            unit = big_job(n)
                        reg = unit[:, (j % pairs) * width:(j % pairs + 1) * width].rearrange("p (h k) -> p h k", h=2)
                        mm(reg, qs[0:KR, j, t * P:(t + 1) * P], ks[0:KR, j, :, b * S:b * S + keys], stop=False)
                        ins = mm(reg[:, :, keys - P:keys], identb[:, :],
                                 mask_q[:, :].unsqueeze(1).broadcast_to([P, 2, P]), start=False)
                        if j % pairs == pairs - 1:
                            ins.then_inc(big_full[n % 3], 1)
                            n += 1
                wait_big_free(pe, n - 1)
                transposes(SMALL0["SAM", g], [negm[:, t, :] for t in range(GT)], rows=H)

            def cross_max(g):
                pe.wait_ge(stack_c, STACK_C * (g + 1))
                for t in range(GT):
                    n = BIG0["CAM", g] + t
                    unit = big_job(n)
                    for j in range(NP):
                        ins = mm(unit[:, j * P:(j + 1) * P], qc[0:KR, j, t * P:(t + 1) * P], kc[0:KR, j, t // 2, :])
                    ins.then_inc(big_full[n % 3], 1)
                wait_big_free(pe, n)
                transposes(SMALL0["CAM", g], [negm[:, t, :] for t in range(GT)], rows=H)

            def self_exp(g):
                pe.wait_ge(m_s, 32 * (g + 1))
                wait_small_free(pe, SMALL0["SAP", g] + 3)

                def scores(p):
                    b, j = p // NP, p % NP
                    n = BIG0["SAE", g] + p
                    unit = big_job(n)
                    for h2 in range(2):
                        reg = unit[:, 512 * h2:512 * (h2 + 1)]
                        at = b * S
                        mm(reg[:, 0:S], ks[0:KM, j, h2, at:at + P], qs[0:KM, j, at:at + S], stop=False)
                        mm(reg[:, S:S + P], ks[0:KM, j, h2, at + P:at + S], qs[0:KM, j, at + P:at + S],
                           start=False, stop=False)
                        ins = mm(reg.rearrange("p (a n) -> p a n", a=2)[:, :, 0:P], identb[:, :],
                                 mask_k[:, :].unsqueeze(1).broadcast_to([P, 2, P]), start=False)
                    ins.then_inc(big_full[n % 3], 1)

                def values(i):
                    b, hg = i // 4, i % 4
                    n = SMALL0["SAE", g] + i
                    bank = small_job(n)
                    wait_big_free(pe, BIG0["SAE", g] + 2 * i)
                    wait_big_free(pe, BIG0["SAE", g] + 2 * i + 1)
                    for kt in range(2):
                        for hh in range(4):
                            e = pt[:, (2 * i + hh // 2) % 4, hh % 2, :]
                            ins = mm(bank[32 * hh:32 * hh + 32, kt * P:S], vaug[:, 2 * b + kt, 4 * hg + hh, :],
                                     e[:, S * kt:S + P * kt], start=(kt == 0), stop=(kt == 1))
                    ins.then_inc(small_full[n % 2], 1)

                for p in range(GB * NP):
                    scores(p)
                    if p % 2 == 1 and p >= 3:
                        values((p - 3) // 2)
                values(GB * NP // 2 - 1)

            def cross_exp(g):
                pe.wait_ge(m_c, 32 * (g + 1))
                wait_small_free(pe, SMALL0["CAP", g] + 3)

                def scores(i):
                    b, jh = i // 2, i % 2
                    n = BIG0["CAE", g] + i
                    unit = big_job(n)
                    for jj in range(4):
                        ins = mm(unit[:, jj * S:(jj + 1) * S], kc[0:KM, 4 * jh + jj, b, :],
                                 qc[0:KM, 4 * jh + jj, b * S:(b + 1) * S])
                    ins.then_inc(big_full[n % 3], 1)

                def values(i):
                    b, jh = i // 2, i % 2
                    n = SMALL0["CAE", g] + i
                    bank = small_job(n)
                    wait_big_free(pe, BIG0["CAE", g] + i)
                    for jj in range(4):
                        ins = mm(bank[32 * jj:32 * jj + 32, 0:S], vblk[:, b, 4 * jh + jj, :], ptc[:, i % 2, jj, :])
                    ins.then_inc(small_full[n % 2], 1)

                for i in range(2 * GB):
                    scores(i)
                    if i > 0:
                        values(i - 1)
                values(2 * GB - 1)

            def output(kind, g):
                last = SMALL0["SAE" if kind == "SAO" else "CAE", g] + SMALL["SAE" if kind == "SAO" else "CAE"] - 1
                wait_small_free(pe, last)
                wait_small_free(pe, last - 1)
                for i in range(BIG[kind]):
                    n = BIG0[kind, g] + i
                    unit = big_job(n)
                    tiles = GT // BIG[kind]
                    for tt in range(tiles):
                        t = tiles * i + tt
                        cols = slice((t % 2) * P, (t % 2 + 1) * P)
                        src = oT[:, t // 2, :, cols] if kind == "SAO" else oTc[:, t // 2, :, cols]
                        blocks = src.shape[1]
                        for a in range(blocks):
                            at = (tt * blocks + a) * P
                            ins = nc.tensor.transpose(unit[:, at:at + P], src[:, a, :], ident[:, :])
                    ins.then_inc(big_full[n % 3], 1)
                for i in range(BIG[kind]):
                    wait_big_free(pe, BIG0[kind, g] + i)
                n = SMALL0[kind, g]
                transposes(n, [o_sb[:, t, :] for t in range(GT)])
                wait_small_free(pe, n)
                bank = small_job(n + 1)
                for t in range(GT):
                    ins = mm(bank[:, t * D:(t + 1) * D], oTn[:, t * P:(t + 1) * P],
                             (sa_sb if kind == "SAO" else ca_sb)[:, 3, :])
                ins.then_inc(small_full[(n + 1) % 2], 1)

            def router(g):
                n = SMALL0["R", g]
                pe.wait_ge(ln_ready, norm_turn["CAO", g] + 1)
                transposes(n, [xs[:, g * GT + t, :] for t in range(GT)])
                wait_small_free(pe, n)
                bank = small_job(n + 1)
                for t in range(GT):
                    ins = mm(bank[:, t * E:(t + 1) * E], x3T[:, g * T + t * P:g * T + (t + 1) * P], rw_sb[:, :])
                ins.then_inc(small_full[(n + 1) % 2], 1)
                pe.wait_ge(comb_ready, g + 1)
                transposes(n + 2, [comb[:, g * GT + t, :] for t in range(GT)], rows=E)
                wait_small_free(pe, n + 2)
                bank = small_job(n + 3)
                for t in range(GT):
                    ins = mm(bank[:, t * D:(t + 1) * D], combT[:, t * P:(t + 1) * P], b2_sb[:, :])
                ins.then_inc(small_full[(n + 3) % 2], 1)

            def up(i):
                g, e = i // E, i % E
                for half in range(2):
                    n = BIG0["MOE", g] + 2 * e + half
                    unit = big_job(n)
                    for c in range(2):
                        f = (2 * half + c) * P
                        ins = mm(unit[:, c * T:(c + 1) * T], w1_sb[:, e, f:f + P], x3T[:, g * T:(g + 1) * T])
                    ins.then_inc(big_full[n % 3], 1)

            def down(i):
                g, e = i // E, i % E
                n = SMALL0["MOE", g] + e
                bank = small_job(n)
                wait_big_free(pe, BIG0["MOE", g] + 2 * e)
                wait_big_free(pe, BIG0["MOE", g] + 2 * e + 1)
                for t in range(GT):
                    for c in range(FC):
                        ins = mm(bank[:, t * D:(t + 1) * D], hid[:, e % 2, c, t * P:(t + 1) * P], w2_sb[:, e, c, :],
                                 start=(c == 0), stop=(c == FC - 1))
                ins.then_inc(small_full[n % 2], 1)

            def experts(g):
                if g == 0:
                    pe.wait_ge(ld_w1, 16)
                    pe.wait_ge(ld_w2, 16)
                    up(0)
                for i in range(g * E, (g + 1) * E):
                    if i + 1 < G * E:
                        up(i + 1)
                    down(i)

            for kind, g in ORDER:
                {"SETUP": setup, "KV": kv, "L0": first_attention, "SAP": self_projections, "SAM": self_max,
                 "SAE": self_exp, "CAP": cross_projections, "CAM": cross_max, "CAE": cross_exp, "R": router,
                 "MOE": experts}.get(kind, lambda g: None)(g)
                if kind in ("SAO", "CAO"):
                    output(kind, g)


def kernel(**inputs):
    import concourse.bacc as bacc
    from concourse.bass_utils import run_bass_kernel_spmd

    a = {n.removeprefix("L1_xattn_"): np.asarray(v)
         for n, v in inputs.items()}
    rows = [a[n] for n in ("sa_bv", "sa_bo", "ca_bv", "ca_bo", "ln1_g", "ln1_b", "ln2_g", "ln2_b", "ln3_g",
                           "ln3_b", "router_b")] + [np.arange(E, dtype=np.float32)]
    arrays = {
        "x": a["x"].reshape(B * S, D),
        "ctx_t": a["ctx_1024"].reshape(B * SC, D).T,
        "wq_t": a["L0_xattn_wq"].T, "wk_t": a["L0_xattn_wk"].T, "wv_t": a["L0_xattn_wv"].T,
        "wo": a["L0_xattn_wo"],
        "norm_w": a["L0_xattn_norm_w"].reshape(D, 1),
        "sa_w": np.stack([a[n] for n in ("sa_wq", "sa_wk", "sa_wv", "sa_wo")]),
        "ca_w": np.stack([a[n] for n in ("ca_wq", "ca_wk", "ca_wv", "ca_wo")]),
        "bqk": np.stack([a[n] for n in ("sa_bq", "sa_bk", "ca_bq", "ca_bk")], axis=1),
        "rows": np.concatenate(rows).reshape(1, -1),
        "router_w": a["router_w"],
        "w1": a["e_w1"],
        "b1": a["e_b1"].reshape(E * FC, P).T,
        "w2": a["e_w2"], "b2": a["e_b2"],
    }
    arrays = {n: np.ascontiguousarray(v) for n, v in arrays.items()}
    nc = bacc.Bacc("TRN2", target_bir_lowering=False, num_devices=1)
    args = [nc.dram_tensor(n, v.shape, mybir.dt.from_np(v.dtype), kind="ExternalInput").ap() for n, v in arrays.items()]
    args.append(nc.dram_tensor("out", (B * S, D), F32, kind="ExternalOutput").ap())
    xattn_layer_kernel(nc, *args)
    r = run_bass_kernel_spmd(nc, [arrays], core_ids=[0])
    return r.results[0]["out"].reshape(B, S, D)
```

```python
from contextlib import ExitStack

import numpy as np
import concourse.bass as bass
from concourse import mybir

F32 = mybir.dt.float32
BF16 = mybir.dt.bfloat16
U32 = mybir.dt.uint32
ALU = mybir.AluOpType
ACT = mybir.ActivationFunctionType
AX = mybir.AxisListType

P = 128
B, S, D = 8, 256, 128
SC = 64
H, DK, HD = 16, 64, 8
E, FF = 8, 512
FC = FF // P
NP = H // 2
G = B
GT = S // P
SLOTS = 6
Q_SLOTS = [(0, 1, 3), (1, 1, 2), (2, 1, 1)]
K_SLOTS = [(0, 3, 1), (0, 2, 1), (0, 1, 1)]
KR = SLOTS * 2 * HD
KM = KR + 4
NEG = -1.0e30
RMS_EPS, LN_EPS = 1e-6, 1e-5
SCALE = float(HD) ** -0.5

NB, NS = 3, 2
BIG = {"LS": 1, "LT": 1, "SM": 1, "SE": 2, "SO": 1, "CM": 1, "CE": 1, "MU": 1}
SMALL = {"FW": 8, "KV": 2, "LX": 1, "LV": 1, "SP": 1, "SQ": 2, "SX": 1, "SV": 1, "ST": 1, "SW": 1,
         "CP": 1, "CQ": 2, "CX": 1, "CV": 1, "CO": 1, "CT": 1, "CW": 1,
         "RX": 1, "RL": 1, "RC": 1, "RB": 1, "MD": 1}


PERIOD = """
LR@0 SW@4 MD.2@6 CO@5 SM.0@3 MU.4@6 SN@4 SM.1@3 SM.2@3 MD.3@6 SM.3@3 CP@4 KV.0@1 CT@5 SM.4@3 CQ@4 SM.5@3
MU.5@6 MD.4@6 KV.1@1 SX@3 MO@7 MU.6@6 CW@5 MD.5@6 LS.0@1 LS.1@1 CN@5 LV.0@2 MU.7@6 MD.6@6 SZ@3 CY@4 LV.1@2
RX@5 SE.0@3 CM.0@4 RL@5 MD.7@6 SE.1@3 SV.0@3 SP@2 CM.1@4 SE.2@3 SV.1@3 SE.3@3 RT@5 CX@4 SV.2@3 CZ@4 MU.0@5
RC@5 SV.3@3 RB@5 SQ@2 MU.1@5 SO@3 MN@6 MD.0@5 CE.0@4 MD.1@5 SY@2 ST@3 CE.1@4 LX@0 MU.2@5 CV.0@4 CV.1@4 MU.3@5
LT.0@1 LT.1@1
"""


def pipeline():
    period = []
    for entry in PERIOD.split():
        step, lag = entry.split("@")
        kind, _, index = step.partition(".")
        period.append((kind, int(index or 0), int(lag)))
    last = G + max(lag for _, _, lag in period)
    steps = [(kind, i - lag, index) for i in range(last) for kind, index, lag in period]
    return [("FW", 0, 0)] + [s for s in steps if 0 <= s[1] < G]


ORDER = pipeline()


def first_jobs(count):
    at, out = 0, {}
    for step in ORDER:
        out[step] = at
        at += count.get(step[0], 0)
    return out


BIG0, SMALL0 = first_jobs(BIG), first_jobs(SMALL)


def xattn_layer_kernel(nc, x, ctx_t, wq_t, wk_t, wv_t, wo, norm_w, sa_w, ca_w, bqk, rows, router_w,
                       w1, b1, w2, b2, out):
    with ExitStack() as stack:
        def sb(name, shape, dt=F32):
            return stack.enter_context(nc.sbuf_tensor(name, shape, dt))

        def sem(name):
            return stack.enter_context(nc.semaphore(name))

        def both(make):
            return {"S": make("s"), "C": make("c")}

        xs = sb("xs", [P, G * GT, D])
        ctxT = sb("ctxT", [P, B * SC])
        fold_w = sb("fold_w", [P, 4, NP, P])
        w1_sb = fold_w[:, :, :, :].rearrange("p a j n -> p (a j n)").rearrange("p (e f) -> p e f", e=E)
        w2_sb = sb("w2_sb", [P, E, FC, D])
        mF = sb("mF", [P, 2, NP, P])
        nF = sb("nF", [P, 2, NP, P])
        normw = sb("normw", [P, 1])
        kf = sb("kf", [P, 2, H * SC])
        vf = sb("vf", [P, 2, NP * P])
        xn = sb("xn", [P, GT, D])
        xnT = sb("xnT", [P, 2, S])
        pr = sb("pr", [P, 2, H * SC])
        prT = sb("prT", [P, 2, NP * P])
        hid = sb("hid", [P, 2, FC, S])
        xT = both(lambda a: sb("xT_" + a, [P, S]))
        split32 = both(lambda a: sb("split32_" + a, [P, 2 * S]))
        parts = both(lambda a: sb("parts_" + a, [P, 3, 2 * S], BF16))
        qs = sb("qs", [P, NP, S], BF16)
        ks = sb("ks", [P, NP, 2, S], BF16)
        qc = sb("qc", [P, NP, S], BF16)
        kc = sb("kc", [P, NP, 2 * SC], BF16)
        negm = both(lambda a: sb("negm_" + a, [P, GT, H]))
        mparts = both(lambda a: sb("mparts_" + a, [H, 2, S], BF16))
        vaug = sb("vaug", [P, GT, H, 32])
        vblk = sb("vblk", [P, NP, 32])
        pt = sb("pt", [P, 4, 2, 384])
        ptc = sb("ptc", [P, 2, 4, S])
        oT = {"S": sb("oT_s", [P, 4, S]), "C": sb("oT_c", [P, 2, S])}
        rsum = both(lambda a: sb("rsum_" + a, [P, GT * H]))
        o_sb = both(lambda a: sb("o_" + a, [P, GT, D]))
        oTn = both(lambda a: sb("oTn_" + a, [P, S]))
        w_sb = both(lambda a: sb("w_" + a, [P, 4, D]))
        bqk_sb = sb("bqk_sb", [P, 4])
        rows_sb = sb("rows_sb", [P, 10 * D + 2 * E])
        bc = rows_sb[:, 0:4 * D].rearrange("p (a d) -> p a d", a=4)
        lnr = rows_sb[:, 4 * D:10 * D].rearrange("p (a d) -> p a d", a=6)
        rb_sb = rows_sb[:, 10 * D:10 * D + E]
        iota = rows_sb[:, 10 * D + E:10 * D + 2 * E]
        rw_sb = sb("rw_sb", [P, E])
        b1_sb = sb("b1_sb", [P, E * FC])
        b2_sb = sb("b2_sb", [E, D])
        x3T = sb("x3T", [P, G * S])
        comb = sb("comb", [P, G * GT, E])
        combT = sb("combT", [E, S])
        ident = sb("ident", [P, P])
        identb = sb("identb", [P, P], BF16)
        mask_q = sb("mask_q", [P, P], BF16)
        mask_k = sb("mask_k", [P, P], BF16)
        mhalf = sb("mhalf", [P, 1])
        norms = ("L", "S", "C", "M")
        st = {a: sb("st_" + a, [P, GT, 6]) for a in norms}
        mv = {a: sb("mv_" + a, [P, GT, 2]) for a in norms}
        var = {a: sb("var_" + a, [P, GT]) for a in norms}
        rstd = {a: sb("rstd_" + a, [P, GT]) for a in norms}
        l0m = sb("l0m", [P, 2, H])
        l0s = sb("l0s", [P, 2, H])
        rt = sb("rt", [P, 6, GT, E])
        rs = sb("rs", [P, 6, GT])
        idx = sb("idx", [P, GT, E], U32)

        big = [stack.enter_context(nc.psum_tensor(f"big{i}", [P, 1024], F32)) for i in range(NB)]
        small = [stack.enter_context(nc.psum_tensor(f"small{i}", [P, 512], F32)) for i in range(NS)]

        q_d = both(lambda a: nc.dram_tensor("q_d_" + a, [G, P, SLOTS, S], BF16, kind="Internal").ap())
        k_d = {a: nc.dram_tensor("k_d_" + a, [G, P, SLOTS, n], BF16, kind="Internal").ap()
               for a, n in (("S", S), ("C", SC))}
        m_d = both(lambda a: nc.dram_tensor("m_d_" + a, [G, H, 2, S], BF16, kind="Internal").ap())

        big_full = [sem(f"big_full{i}") for i in range(NB)]
        big_free = [sem(f"big_free{i}") for i in range(NB)]
        small_full = [sem(f"small_full{i}") for i in range(NS)]
        small_free = [sem(f"small_free{i}") for i in range(NS)]
        ld_x, ld_ctx, ld_fold, ld_layer = sem("ld_x"), sem("ld_ctx"), sem("ld_fold"), sem("ld_layer")
        ld_w1, ld_w2 = sem("ld_w1"), sem("ld_w2")
        consts_ready = sem("consts_ready")
        zeros_ready = sem("zeros_ready")
        bias_ready = sem("bias_ready")
        ones_ready = sem("ones_ready")
        dve_step = sem("dve_step")
        pool_step = sem("pool_step")
        var_ready = sem("var_ready")
        rstd_ready = sem("rstd_ready")
        xn_ready = sem("xn_ready")
        exp_ready = sem("exp_ready")
        rec_ready = sem("rec_ready")
        probs_ready = sem("probs_ready")
        qk_ready = sem("qk_ready")
        parts_ready = both(lambda a: sem("parts_ready_" + a))
        parts_stored = both(lambda a: sem("parts_stored_" + a))
        stacked = both(lambda a: sem("stacked_" + a))
        m_stored = both(lambda a: sem("m_stored_" + a))
        m_rows = both(lambda a: sem("m_rows_" + a))
        ln_ready = both(lambda a: sem("ln_ready_" + a))
        logit_ready = sem("logit_ready")
        rexp_ready = sem("rexp_ready")
        comb_ready = sem("comb_ready")
        res_ready = sem("res_ready")
        out_done = sem("out_done")

        def wait_big_full(eng, n):
            eng.wait_ge(big_full[n % NB], n // NB + 1)

        def wait_big_free(eng, n):
            if n >= 0:
                eng.wait_ge(big_free[n % NB], n // NB + 1)

        def wait_small_full(eng, n):
            eng.wait_ge(small_full[n % NS], n // NS + 1)

        def wait_small_free(eng, n):
            if n >= 0:
                eng.wait_ge(small_free[n % NS], n // NS + 1)

        STORED, STACKED = 16 * 6, 16 * 3
        CK = {"S": S, "C": SC}

        def turn(*kinds):
            return {s: i for i, s in enumerate(s for s in ORDER if s[0] in kinds)}

        var_turn, qk_turn = turn("LR", "SW", "CW", "MN"), turn("SQ", "CQ")

        block = stack.enter_context(nc.Block())

        @block.sync
        def _(sp):
            sp.dma_start(fold_w[:, 0], wq_t.rearrange("(j p) n -> p j n", p=P)).then_inc(ld_fold, 16)
            sp.dma_start(ctxT[:, :], ctx_t).then_inc(ld_ctx, 16)
            sp.dma_start(fold_w[:, 2], wv_t.rearrange("(j p) n -> p j n", p=P)).then_inc(ld_fold, 16)
            sp.dma_start(normw[:, :], norm_w).then_inc(ld_fold, 16)
            sp.dma_start(w_sb["S"][:, :, :], sa_w.rearrange("a d n -> d a n")).then_inc(ld_layer, 16)
            sp.dma_start(bqk_sb[:, :], bqk).then_inc(ld_layer, 16)
            sp.dma_start(rows_sb[:, :], rows.broadcast_to([P, 10 * D + 2 * E])).then_inc(ld_layer, 16)
            sp.dma_start(w_sb["C"][:, :, :], ca_w.rearrange("a d n -> d a n")).then_inc(ld_layer, 16)
            sp.dma_start(rw_sb[:, :], router_w).then_inc(ld_layer, 16)
            sp.dma_start(b1_sb[:, :], b1).then_inc(ld_layer, 16)
            sp.dma_start(b2_sb[:, :], b2).then_inc(ld_layer, 16)
            sp.dma_start(w2_sb[:, :, :, :], w2.rearrange("e (c p) n -> p e c n", p=P)).then_inc(ld_w2, 16)

            def store_parts(a, g):
                sp.wait_ge(parts_ready[a], g + 1)
                for dram, cols, slots in ((q_d[a], slice(0, S), Q_SLOTS), (k_d[a], slice(S, S + CK[a]), K_SLOTS)):
                    at = 0
                    for first, count, times in slots:
                        src = parts[a][:, first:first + count, cols]
                        if times > 1:
                            src = src.broadcast_to([P, times, S])
                        sp.dma_start(dram[g, :, at:at + count * times, :], src).then_inc(parts_stored[a], 16)
                        at += count * times

            def stack_parts(a, g):
                sp.wait_ge(parts_stored[a], STORED * (g + 1))
                if g > 0 and a == "S":
                    wait_big_full(sp, BIG0["SE", g - 1, 3] + 1)
                if g > 0 and a == "C":
                    wait_big_full(sp, BIG0["CE", g - 1, 1])
                q, k = (qs, ks) if a == "S" else (qc, kc.rearrange("p j (h t) -> p j h t", h=2))
                sp.dma_start(q[0:KR, :, :], q_d[a][g].rearrange("(j r) s t -> (r s) j t", j=NP)).then_inc(stacked[a], 16)
                for h2 in range(2):
                    src = k_d[a][g].rearrange("(j h d) s t -> h (d s) j t", j=NP, h=2)[h2]
                    sp.dma_start(k[KR // 2 * h2:KR // 2 * (h2 + 1), :, h2, :], src).then_inc(stacked[a], 16)

            def store_maxima(a, g):
                wait_small_free(sp, SMALL0[a + "X", g, 0])
                sp.dma_start(m_d[a][g], mparts[a][:, :, :]).then_inc(m_stored[a], 16)

            def maxima_rows(a, g):
                sp.wait_ge(m_stored[a], 16 * (g + 1))
                for part in range(2):
                    src = m_d[a][g, :, part, :].rearrange("(j h) t -> h j t", j=NP)
                    sp.dma_start((qs if a == "S" else qc)[KR + 2 * part:KR + 2 * part + 2, :, :], src).then_inc(
                        m_rows[a], 16)

            for kind, g, i in ORDER:
                if kind == "FW":
                    wait_small_full(sp, SMALL0["FW", 0, 0] + 7)
                    wait_small_full(sp, SMALL0["FW", 0, 0] + 6)
                    sp.dma_start(w1_sb, w1.rearrange("e d f -> d e f")).then_inc(ld_w1, 16)
                if kind in ("SQ", "CQ"):
                    store_parts(kind[0], g)
                if kind in ("SY", "CY"):
                    stack_parts(kind[0], g)
                if kind in ("SX", "CX"):
                    store_maxima(kind[0], g)
                if kind in ("SZ", "CZ"):
                    maxima_rows(kind[0], g)
                if kind == "MO":
                    sp.wait_ge(res_ready, g + 1)
                    sp.dma_start(out.rearrange("(t p) d -> p t d", p=P)[:, g * GT:(g + 1) * GT],
                                 xs[:, g * GT:(g + 1) * GT, :]).then_inc(out_done, 16)
            sp.wait_ge(out_done, 16 * G)

        @block.gpsimd
        def _(pool):
            steps = [0]

            def step(ins):
                steps[0] += 1
                ins.then_inc(pool_step, 1)
                pool.wait_ge(pool_step, steps[0])

            def diagonal(m, pattern, multiplier, op, fill):
                step(nc.gpsimd.memset(m[:, :], 0.0))
                nc.gpsimd.affine_select(out=m[:, :], in_=m[:, :], compare_op=op, fill=fill, base=0,
                                        pattern=pattern, channel_multiplier=multiplier).then_inc(consts_ready, 1)

            diagonal(ident, [[-1, P]], 1, ALU.not_equal, 1.0)
            diagonal(identb, [[-1, P]], 1, ALU.not_equal, 1.0)
            diagonal(mask_q, [[-1, P]], 1, ALU.is_ge, NEG)
            diagonal(mask_k, [[1, P]], -1, ALU.is_ge, NEG)

            def ones_rows(rows4, pattern):
                for base in (0, -2):
                    ins = nc.gpsimd.affine_select(out=rows4, in_=rows4, compare_op=ALU.not_equal, fill=1.0,
                                                  base=base, pattern=pattern, channel_multiplier=1)
                    if base == 0:
                        step(ins)
                ins.then_inc(ones_ready, 1)

            pool.wait_ge(zeros_ready, 1)
            pool.wait_ge(consts_ready, 4)
            ones_rows(ks[KR:KM, :, :, :], [[0, NP], [-1, 2], [0, S]])
            pool.wait_ge(ones_ready, 1)
            ones_rows(kc[KR:KM, :, :].rearrange("p j (h k) -> p j h k", h=2), [[0, NP], [-1, 2], [0, SC]])
            pool.wait_ge(ones_ready, 2)

            for kind, g, i in ORDER:
                if kind in ("LR", "SW", "CW", "MN"):
                    n = var_turn[kind, g, i]
                    pool.wait_ge(var_ready, n + 1)
                    nc.gpsimd.tensor_tensor(rstd[kind[0]][:, :], var[kind[0]][:, :],
                                            mhalf[:, :].broadcast_to([P, GT]), ALU.pow).then_inc(rstd_ready, 1)
                if kind == "LT":
                    pool.wait_ge(rec_ready, GT * g + i + 1)
                    pv = pr[:, i % 2, :].rearrange("p (h k) -> p h k", h=H)
                    nc.gpsimd.tensor_tensor(pv, pv, l0s[:, i % 2, :].unsqueeze(2).broadcast_to([P, H, SC]),
                                            ALU.mult).then_inc(probs_ready, 1)

        @block.scalar
        def _(act):
            act.dma_start(fold_w[:, 1], wk_t.rearrange("(j p) n -> p j n", p=P)).then_inc(ld_fold, 16)
            act.dma_start(fold_w[:, 3], wo.rearrange("(j p) n -> p j n", p=P)).then_inc(ld_fold, 16)
            act.dma_start(xs[:, :, :], x.rearrange("(t p) d -> p t d", p=P)).then_inc(ld_x, 16)

            def copy_small(n, dst, width):
                wait_small_full(act, n)
                nc.scalar.copy(dst, small[n % NS][:, 0:width]).then_inc(small_free[n % NS], 1)

            for kind, g, i in ORDER:
                a = kind[0]
                n, m = SMALL0[kind, g, i], BIG0[kind, g, i]
                if kind == "FW":
                    for k in range(4):
                        copy_small(n + k, mF[:, k % 2, 4 * (k // 2):4 * (k // 2) + 4, :], 512)
                if kind == "KV":
                    wait_small_full(act, n)
                    nc.scalar.activation(kf[:, g % 2, :].rearrange("p (j h k) -> p h j k", j=NP, h=2)[:, i],
                                         small[n % NS][:, :].rearrange("p (j k) -> p j k", j=NP),
                                         ACT.Copy, scale=normw[:, 0:1]).then_inc(small_free[n % NS], 1)
                if kind == "LX":
                    copy_small(n, xnT[:, g % 2, :], S)
                if kind == "LS":
                    wait_big_free(act, m)
                    nc.scalar.activation(pr[:, i % 2, :], pr[:, i % 2, :], ACT.Exp).then_inc(exp_ready, 1)
                if kind == "LT":
                    wait_big_full(act, m)
                    nc.scalar.copy(prT[:, i % 2, :], big[m % NB][:, :]).then_inc(big_free[m % NB], 1)
                if kind in ("SP", "CP"):
                    copy_small(n, xT[a][:, :], S)
                if kind in ("SQ", "CQ"):
                    if g == 0:
                        act.wait_ge(bias_ready, 1)
                    else:
                        act.wait_ge(parts_ready[a], g)
                    c = 0 if a == "S" else 2
                    wait_small_full(act, n)
                    nc.scalar.activation(split32[a][:, 0:S], small[n % NS][:, 0:S], ACT.Identity,
                                         bias=bqk_sb[:, c:c + 1], scale=SCALE)
                    nc.scalar.activation(split32[a][:, S:S + CK[a]], small[n % NS][:, S:S + CK[a]], ACT.Identity,
                                         bias=bqk_sb[:, c + 1:c + 2]).then_inc(small_free[n % NS], 1)
                if kind == "SE":
                    for k in range(2):
                        wait_big_full(act, m + k)
                        nc.scalar.activation(pt[:, (2 * i + k) % 4, :, :],
                                             big[(m + k) % NB][:, :].rearrange("p (h n) -> p h n", h=2)[:, :, 0:384],
                                             ACT.Exp).then_inc(big_free[(m + k) % NB], 1)
                if kind == "CE":
                    wait_big_full(act, m)
                    nc.scalar.activation(ptc[:, i % 2], big[m % NB][:, :].rearrange("p (j q) -> p j q", j=4),
                                         ACT.Exp).then_inc(big_free[m % NB], 1)
                if kind == "CV":
                    copy_small(n, oT["C"][:, i, :], S)
                if kind in ("ST", "CT"):
                    copy_small(n, oTn[a][:, :], S)
                if kind == "RX":
                    copy_small(n, x3T[:, g * S:(g + 1) * S], S)
                if kind == "RL":
                    act.wait_ge(logit_ready, 2 * g + 1)
                    nc.scalar.activation(rt[:, 1, :, :], rt[:, 0, :, :], ACT.Exp).then_inc(rexp_ready, 1)
                if kind == "RT":
                    act.wait_ge(logit_ready, 2 * g + 2)
                    nc.scalar.activation(rs[:, 3, :], rs[:, 2, :], ACT.Exp).then_inc(rexp_ready, 1)
                if kind == "MU":
                    wait_big_full(act, m)
                    for c in range(FC):
                        ins = nc.scalar.activation(hid[:, i % 2, c, :], big[m % NB][:, c * S:(c + 1) * S],
                                                   ACT.Gelu, bias=b1_sb[:, i * FC + c:i * FC + c + 1])
                    ins.then_inc(big_free[m % NB], 1)

        @block.vector
        def _(dve):
            steps = [0]

            def step(ins):
                steps[0] += 1
                ins.then_inc(dve_step, 1)
                dve.wait_ge(dve_step, steps[0])

            def fold(g):
                nc.vector.memset(ks[:, :, :, :].bitcast(U32), 0)
                nc.vector.memset(kc[:, :, :].bitcast(U32), 0)
                nc.vector.memset(mhalf[:, :], -0.5).then_inc(zeros_ready, 1)
                nc.vector.memset(vaug[:, :, :, :], 0.0)
                step(nc.vector.memset(vblk[:, :, :], 0.0))
                nc.vector.memset(vaug[:, :, :, HD:HD + 1], 1.0)
                nc.vector.memset(vblk[0:SC, :, HD:HD + 1], 1.0)
                nc.vector.memset(vblk[SC:P, :, 16 + HD:16 + HD + 1], 1.0)
                for i in range(4):
                    n = SMALL0["FW", 0, 0] + 4 + i
                    wait_small_full(dve, n)
                    nc.vector.tensor_copy(nF[:, i % 2, 4 * (i // 2):4 * (i // 2) + 4, :],
                                          small[n % NS][:, :]).then_inc(small_free[n % NS], 1)
                dve.wait_ge(ld_layer, 16 * 7)
                q_bias = bqk_sb[:, :].rearrange("p (a b) -> p a b", a=2)[:, :, 0]
                nc.vector.tensor_scalar(q_bias, q_bias, SCALE, None, ALU.mult).then_inc(bias_ready, 1)

            def group(g):
                return xs[:, g * GT:(g + 1) * GT, :]

            def copy_small(n, dst, width):
                wait_small_full(dve, n)
                nc.vector.tensor_copy(dst, small[n % NS][:, 0:width]).then_inc(small_free[n % NS], 1)

            def rms(g):
                if g == 0:
                    dve.wait_ge(ld_x, 16)
                else:
                    wait_small_full(dve, SMALL0["LX", g - 1, 0])
                step(nc.vector.tensor_tensor(xn[:, :, :], group(g), group(g), ALU.mult))
                step(nc.vector.reduce_sum(var["L"][:, :], xn[:, :, :], AX.X))
                nc.vector.tensor_scalar(var["L"][:, :], var["L"][:, :], 1.0 / D, RMS_EPS, ALU.mult,
                                        ALU.add).then_inc(var_ready, 1)

            def normed(g):
                dve.wait_ge(rstd_ready, var_turn["LR", g, 0] + 1)
                nc.vector.tensor_tensor(xn[:, :, :], group(g), rstd["L"][:, :].unsqueeze(2).broadcast_to([P, GT, D]),
                                        ALU.mult).then_inc(xn_ready, 1)

            def scores(g, t):
                n = BIG0["LS", g, t]
                wait_big_full(dve, n)
                s = big[n % NB][:, :].rearrange("p (h k) -> p h k", h=H)
                step(nc.vector.reduce_max(l0m[:, t % 2, :], s, AX.X, negate=True))
                nc.vector.tensor_tensor(pr[:, t % 2, :].rearrange("p (h k) -> p h k", h=H), s,
                                        l0m[:, t % 2, :].unsqueeze(2).broadcast_to([P, H, SC]),
                                        ALU.add).then_inc(big_free[n % NB], 1)

            def sums(g, t):
                dve.wait_ge(exp_ready, GT * g + t + 1)
                step(nc.vector.reduce_sum(l0s[:, t % 2, :], pr[:, t % 2, :].rearrange("p (h k) -> p h k", h=H), AX.X))
                nc.vector.reciprocal(l0s[:, t % 2, :], l0s[:, t % 2, :]).then_inc(rec_ready, 1)

            def first_residual(g, t):
                n = SMALL0["LV", g, t]
                wait_small_full(dve, n)
                nc.vector.tensor_tensor(xs[:, g * GT + t, :], xs[:, g * GT + t, :], small[n % NS][:, 0:D],
                                        ALU.add).then_inc(small_free[n % NS], 1)

            def split(a, g):
                width = S + CK[a]
                n = SMALL0[a + "Q", g, 0]
                q = split32[a][:, 0:width]
                part = [parts[a][:, i, 0:width] for i in range(NB)]
                wait_small_free(dve, n)
                if g > 0:
                    dve.wait_ge(parts_stored[a], 16 * g)
                step(nc.vector.tensor_copy(part[0], q))
                step(nc.vector.tensor_tensor(q, q, part[0], ALU.subtract))
                step(nc.vector.tensor_copy(part[1], q))
                nc.vector.tensor_tensor(part[2], q, part[1], ALU.subtract).then_inc(parts_ready[a], 1)

            def self_values(g):
                n = SMALL0["SQ", g, 0] + 1
                wait_small_full(dve, n)
                for t in range(GT):
                    ins = nc.vector.tensor_tensor(vaug[:, t, :, 0:HD],
                                                  small[n % NS][:, t * D:(t + 1) * D].rearrange("p (h d) -> p h d", h=H),
                                                  bc[:, 0, :].rearrange("p (h d) -> p h d", h=H), ALU.add)
                ins.then_inc(small_free[n % NS], 1)

            def cross_values(g):
                n = SMALL0["CQ", g, 0] + 1
                wait_small_full(dve, n)
                for h2 in range(2):
                    half = slice(h2 * SC, (h2 + 1) * SC)
                    ins = nc.vector.tensor_tensor(
                        vblk[half, :, 16 * h2:16 * h2 + HD],
                        small[n % NS][half, 0:64].rearrange("p (j d) -> p j d", j=NP),
                        bc[half, 2, :].rearrange("p (j h d) -> p h j d", j=NP, h=2)[:, h2], ALU.add)
                ins.then_inc(small_free[n % NS], 1)

            def maximum(n, dst, keys):
                wait_big_full(dve, n)
                nc.vector.reduce_max(dst, big[n % NB][:, :].rearrange("p (h k) -> p h k", k=keys), AX.X,
                                     negate=True).then_inc(big_free[n % NB], 1)

            def max_parts(a, g):
                n = SMALL0[a + "X", g, 0]
                wait_small_full(dve, n)
                if g > 0:
                    dve.wait_ge(m_stored[a], 16 * g)
                step(nc.vector.tensor_copy(mparts[a][:, 0, :], small[n % NS][0:H, 0:S]))
                nc.vector.tensor_tensor(mparts[a][:, 1, :], small[n % NS][0:H, 0:S], mparts[a][:, 0, :],
                                        ALU.subtract).then_inc(small_free[n % NS], 1)

            def divide(a, g, psum, free, stride):
                o = psum.rearrange("p (h c) -> p h c", c=stride)
                step(nc.vector.reciprocal(rsum[a][:, :], o[:, :, HD]))
                nc.vector.tensor_tensor(o_sb[a][:, :, :].rearrange("p t (h d) -> p (t h) d", h=H), o[:, :, 0:HD],
                                        rsum[a][:, :].unsqueeze(2).broadcast_to([P, GT * H, HD]),
                                        ALU.mult).then_inc(free, 1)

            def norm_statistics(a, g):
                for t in range(GT):
                    ins = nc.vector.bn_stats(st[a][:, t, :], xs[:, g * GT + t, :])
                step(ins)
                for t in range(GT):
                    ins = nc.vector.bn_aggr(mv[a][:, t, :], st[a][:, t, :])
                step(ins)
                nc.vector.tensor_scalar(var[a][:, :], mv[a][:, :, 1], LN_EPS, None, ALU.add).then_inc(var_ready, 1)

            def residual(a, g):
                n = SMALL0[a + "W", g, 0]
                wait_small_full(dve, n)
                nc.vector.tensor_tensor(group(g), group(g), small[n % NS][:, 0:S].rearrange("p (t d) -> p t d", t=GT),
                                        ALU.add).then_inc(small_free[n % NS], 1)
                wait_small_free(dve, n)
                bo = bc[:, 1 if a == "S" else 3, :]
                step(nc.vector.tensor_tensor(group(g), group(g), bo.unsqueeze(1).broadcast_to([P, GT, D]), ALU.add))
                norm_statistics(a, g)

            def layernorm(a, g, kind, which, done):
                dve.wait_ge(rstd_ready, var_turn[kind, g, 0] + 1)
                for t in range(GT):
                    ins = nc.vector.tensor_scalar(xs[:, g * GT + t, :], xs[:, g * GT + t, :], mv[a][:, t, 0:1],
                                                  rstd[a][:, t:t + 1], ALU.subtract, ALU.mult)
                step(ins)
                gain, shift = (lnr[:, 2 * which + i, :].unsqueeze(1).broadcast_to([P, GT, D]) for i in range(2))
                step(nc.vector.tensor_tensor(group(g), group(g), gain, ALU.mult))
                nc.vector.tensor_tensor(group(g), group(g), shift, ALU.add).then_inc(done, 1)

            def col(ap):
                return ap.unsqueeze(2).broadcast_to([P, GT, E])

            def row(ap):
                return ap.unsqueeze(1).broadcast_to([P, GT, E])

            logits, prob, eq1, eq2, m8, idf = (rt[:, k] for k in range(6))
            neg, inv, dif, e2, w_1, w_2 = (rs[:, k, :] for k in range(6))

            def router_logits(g):
                n = SMALL0["RL", g, 0]
                wait_small_full(dve, n)
                nc.vector.tensor_tensor(logits, small[n % NS][:, 0:GT * E].rearrange("p (t e) -> p t e", t=GT),
                                        row(rb_sb), ALU.add).then_inc(small_free[n % NS], 1)
                wait_small_free(dve, n)
                step(nc.vector.reduce_max(neg, logits, AX.X, negate=True))
                nc.vector.tensor_tensor(logits, logits, col(neg), ALU.add).then_inc(logit_ready, 1)

            def router_top2(g):
                dve.wait_ge(rexp_ready, 2 * g + 1)
                step(nc.vector.reduce_sum(inv, prob, AX.X))
                step(nc.vector.reciprocal(inv, inv))
                step(nc.vector.tensor_tensor(prob, prob, col(inv), ALU.mult))
                for t in range(GT):
                    ins = nc.vector.max(m8[:, t, :], prob[:, t, :])
                step(ins)
                nc.vector.tensor_tensor(dif, m8[:, :, 1], m8[:, :, 0], ALU.subtract).then_inc(logit_ready, 1)
                for t in range(GT):
                    ins = nc.vector.max_index(idx[:, t, :], m8[:, t, :], prob[:, t, :])
                step(ins)
                step(nc.vector.tensor_copy(idf, idx[:, :, :]))

            def router_combine(g):
                dve.wait_ge(rexp_ready, 2 * g + 2)
                nc.vector.tensor_tensor(eq1, row(iota), col(idf[:, :, 0]), ALU.is_equal)
                nc.vector.tensor_tensor(eq2, row(iota), col(idf[:, :, 1]), ALU.is_equal)
                step(nc.vector.tensor_scalar(w_1, e2, 1.0, None, ALU.add))
                step(nc.vector.reciprocal(w_1, w_1))
                step(nc.vector.tensor_tensor(w_2, e2, w_1, ALU.mult))
                nc.vector.tensor_tensor(eq1, eq1, col(w_1), ALU.mult)
                step(nc.vector.tensor_tensor(eq2, eq2, col(w_2), ALU.mult))
                nc.vector.tensor_tensor(comb[:, g * GT:(g + 1) * GT, :], eq1, eq2, ALU.add).then_inc(comb_ready, 1)
                n = SMALL0["RC", g, 0]
                wait_small_full(dve, n)
                nc.vector.tensor_copy(combT[:, :], small[n % NS][0:E, 0:S]).then_inc(small_free[n % NS], 1)

            def expert_bias(g):
                n = SMALL0["RB", g, 0]
                wait_small_full(dve, n)
                nc.vector.tensor_tensor(group(g), group(g), small[n % NS][:, 0:S].rearrange("p (t d) -> p t d", t=GT),
                                        ALU.add).then_inc(small_free[n % NS], 1)

            def expert(g, e):
                n = SMALL0["MD", g, e]
                wait_small_full(dve, n)
                wait_small_free(dve, SMALL0["MD", g, e - 1] if e > 0 else SMALL0["RB", g, 0])
                for t in range(GT):
                    ins = nc.vector.scalar_tensor_tensor(
                        xs[:, g * GT + t, :], small[n % NS][:, t * D:(t + 1) * D], comb[:, g * GT + t, e:e + 1],
                        xs[:, g * GT + t, :], ALU.mult, ALU.add)
                ins.then_inc(small_free[n % NS], 1)

            for kind, g, i in ORDER:
                a = kind[0]
                n, m = SMALL0[kind, g, i], BIG0[kind, g, i]
                if kind == "FW":
                    fold(g)
                if kind == "KV":
                    copy_small(n + 1, vf[:, g % 2, i * 512:(i + 1) * 512], 512)
                if kind == "LR":
                    rms(g)
                if kind == "LX":
                    normed(g)
                if kind == "LS":
                    scores(g, i)
                if kind == "LT":
                    sums(g, i)
                if kind == "LV":
                    first_residual(g, i)
                if kind == "SQ":
                    split("S", g)
                    self_values(g)
                if kind == "CQ":
                    split("C", g)
                    cross_values(g)
                if kind == "SM":
                    maximum(m, negm["S"][:, 0, 8 * i:8 * i + 8] if i < 2 else negm["S"][:, 1, 4 * (i - 2):4 * (i - 1)],
                            P if i < 2 else 2 * P)
                if kind == "CM":
                    maximum(m, negm["C"][:, i, :], SC)
                if kind in ("SX", "CX"):
                    max_parts(a, g)
                if kind == "SV":
                    copy_small(n, oT["S"][:, i, :], S)
                if kind == "SO":
                    wait_big_full(dve, m)
                    divide("S", g, big[m % NB][:, :], big_free[m % NB], 32)
                if kind == "CO":
                    wait_small_full(dve, n)
                    divide("C", g, small[n % NS][:, :], small_free[n % NS], 16)
                if kind in ("SW", "CW"):
                    residual(a, g)
                if kind == "SN":
                    layernorm("S", g, "SW", 0, ln_ready["S"])
                if kind == "CN":
                    layernorm("C", g, "CW", 1, ln_ready["C"])
                if kind == "RL":
                    router_logits(g)
                if kind == "RT":
                    router_top2(g)
                if kind == "RC":
                    router_combine(g)
                if kind == "RB":
                    expert_bias(g)
                if kind == "MD":
                    expert(g, i)
                if kind == "MN":
                    wait_small_free(dve, SMALL0["MD", g, E - 1])
                    norm_statistics("M", g)
                if kind == "MO":
                    layernorm("M", g, "MN", 2, res_ready)

        @block.tensor
        def _(pe):
            def mm(out_, lhsT, rhs, start=True, stop=True):
                return nc.tensor.matmul(out_, lhsT, rhs, start=start, stop=stop)

            def small_job(n):
                wait_small_free(pe, n - NS)
                return small[n % NS]

            def big_job(n):
                wait_big_free(pe, n - NB)
                return big[n % NB]

            def fold():
                pe.wait_ge(ld_fold, 16 * 5)
                for i in range(8):
                    n = SMALL0["FW", 0, 0] + i
                    bank = small_job(n)
                    h2, j0 = i % 2, 4 * (i % 4 // 2)
                    a, b = (1, 0) if i < 4 else (2, 3)
                    half = slice(64 * h2, 64 * h2 + 64)
                    for jj in range(4):
                        ins = mm(bank[:, jj * P:(jj + 1) * P], fold_w[half, a, j0 + jj, :], fold_w[half, b, j0 + jj, :])
                    ins.then_inc(small_full[n % NS], 1)
                pe.wait_ge(ld_ctx, 16)
                wait_small_free(pe, SMALL0["FW", 0, 0] + 3)
                wait_small_free(pe, SMALL0["FW", 0, 0] + 7)

            def keys_values(g, i, n):
                bank = small_job(n)
                ctx = ctxT[:, g * SC:(g + 1) * SC]
                for j in range(NP):
                    ins = mm(bank[:, j * SC:(j + 1) * SC], mF[:, i, j, :], ctx)
                ins.then_inc(small_full[n % NS], 1)
                n += 1
                bank = small_job(n)
                for h2 in range(2):
                    ins = mm(bank[64 * h2:64 * h2 + 64, :], ctx, nF[:, h2, 4 * i:4 * i + 4, :])
                ins.then_inc(small_full[n % NS], 1)

            def transposes(n, sources, rows=P):
                bank = small_job(n)
                for t, src in enumerate(sources):
                    ins = nc.tensor.transpose(bank[0:rows, t * P:(t + 1) * P], src, ident[:, :])
                ins.then_inc(small_full[n % NS], 1)

            def tiles(g):
                return [xs[:, g * GT + t, :] for t in range(GT)]

            def first_scores(g, t):
                if t == 0:
                    wait_small_free(pe, SMALL0["LX", g, 0])
                    wait_small_free(pe, SMALL0["KV", g, 1])
                    wait_small_free(pe, SMALL0["KV", g, 1] + 1)
                n = BIG0["LS", g, t]
                unit = big_job(n)
                for i in range(2):
                    ins = mm(unit[:, i * 512:(i + 1) * 512], xnT[:, g % 2, t * P:(t + 1) * P],
                             kf[:, g % 2, i * 512:(i + 1) * 512])
                ins.then_inc(big_full[n % NB], 1)

            def transpose_probs(g, t):
                n = BIG0["LT", g, t]
                unit = big_job(n)
                pe.wait_ge(probs_ready, GT * g + t + 1)
                for j in range(NP):
                    ins = nc.tensor.transpose(unit[:, j * P:(j + 1) * P], pr[:, t % 2, j * P:(j + 1) * P], ident[:, :])
                ins.then_inc(big_full[n % NB], 1)

            def first_values(g, t):
                n = SMALL0["LV", g, t]
                bank = small_job(n)
                wait_big_free(pe, BIG0["LT", g, t])
                for j in range(NP):
                    ins = mm(bank[:, 0:D], prT[:, t % 2, j * P:(j + 1) * P], vf[:, g % 2, j * P:(j + 1) * P],
                             start=(j == 0), stop=(j == NP - 1))
                ins.then_inc(small_full[n % NS], 1)

            def self_projections(g, n):
                wait_small_free(pe, SMALL0["SP", g, 0])
                bank = small_job(n)
                for i in range(2):
                    ins = mm(bank[:, i * S:(i + 1) * S], w_sb["S"][:, i, :], xT["S"][:, :])
                ins.then_inc(small_full[n % NS], 1)
                n += 1
                bank = small_job(n)
                for t in range(GT):
                    ins = mm(bank[:, t * D:(t + 1) * D], xT["S"][:, t * P:(t + 1) * P], w_sb["S"][:, 2, :])
                ins.then_inc(small_full[n % NS], 1)

            def cross_projections(g, n):
                wait_small_free(pe, SMALL0["CP", g, 0])
                ctx = ctxT[:, g * SC:(g + 1) * SC]
                bank = small_job(n)
                mm(bank[:, 0:S], w_sb["C"][:, 0, :], xT["C"][:, :])
                mm(bank[:, S:S + SC], w_sb["C"][:, 1, :], ctx).then_inc(small_full[n % NS], 1)
                n += 1
                bank = small_job(n)
                for h2 in range(2):
                    ins = mm(bank[64 * h2:64 * h2 + 64, 0:64], ctx,
                             w_sb["C"][:, 2, :].rearrange("p (j h d) -> p h j d", j=NP, h=2)[:, h2])
                ins.then_inc(small_full[n % NS], 1)

            def self_max(g, i):
                if i == 0:
                    pe.wait_ge(stacked["S"], STACKED * (g + 1))
                    if g == 0:
                        pe.wait_ge(ones_ready, 2)
                n = BIG0["SM", g, i]
                unit = big_job(n)
                t = 0 if i < 2 else 1
                keys, pairs = P * (t + 1), 4 // (t + 1)
                for jj in range(pairs):
                    j = jj + pairs * (i if i < 2 else i - 2)
                    reg = unit[:, jj * 2 * keys:(jj + 1) * 2 * keys].rearrange("p (h k) -> p h k", h=2)
                    mm(reg, qs[0:KR, j, t * P:(t + 1) * P], ks[0:KR, j, :, 0:keys], stop=False)
                    ins = mm(reg[:, :, keys - P:keys], identb[:, :],
                             mask_q[:, :].unsqueeze(1).broadcast_to([P, 2, P]), start=False)
                ins.then_inc(big_full[n % NB], 1)

            def cross_max(g, t):
                if t == 0:
                    pe.wait_ge(stacked["C"], STACKED * (g + 1))
                n = BIG0["CM", g, t]
                unit = big_job(n)
                for j in range(NP):
                    ins = mm(unit[:, j * P:(j + 1) * P], qc[0:KR, j, t * P:(t + 1) * P], kc[0:KR, j, :])
                ins.then_inc(big_full[n % NB], 1)

            def self_scores(g, i):
                if i == 0:
                    pe.wait_ge(m_rows["S"], 32 * (g + 1))
                for j in (2 * i, 2 * i + 1):
                    n = BIG0["SE", g, i] + j - 2 * i
                    unit = big_job(n)
                    for h2 in range(2):
                        reg = unit[:, 512 * h2:512 * (h2 + 1)]
                        mm(reg[:, 0:S], ks[0:KM, j, h2, 0:P], qs[0:KM, j, 0:S], stop=False)
                        mm(reg[:, S:S + P], ks[0:KM, j, h2, P:S], qs[0:KM, j, P:S], start=False, stop=False)
                        ins = mm(reg.rearrange("p (a n) -> p a n", a=2)[:, :, 0:P], identb[:, :],
                                 mask_k[:, :].unsqueeze(1).broadcast_to([P, 2, P]), start=False)
                    ins.then_inc(big_full[n % NB], 1)

            def self_values(g, i, n):
                if i == 0:
                    wait_small_free(pe, SMALL0["SQ", g, 0] + 1)
                bank = small_job(n)
                wait_big_free(pe, BIG0["SE", g, i])
                wait_big_free(pe, BIG0["SE", g, i] + 1)
                for kt in range(2):
                    for hh in range(4):
                        e = pt[:, (2 * i + hh // 2) % 4, hh % 2, :]
                        ins = mm(bank[32 * hh:32 * hh + 32, kt * P:S], vaug[:, kt, 4 * i + hh, :],
                                 e[:, S * kt:S + P * kt], start=(kt == 0), stop=(kt == 1))
                ins.then_inc(small_full[n % NS], 1)

            def cross_scores(g, i):
                if i == 0:
                    pe.wait_ge(m_rows["C"], 32 * (g + 1))
                n = BIG0["CE", g, i]
                unit = big_job(n)
                for jj in range(4):
                    ins = mm(unit[:, jj * S:(jj + 1) * S], kc[0:KM, 4 * i + jj, :], qc[0:KM, 4 * i + jj, :])
                ins.then_inc(big_full[n % NB], 1)

            def cross_values(g, i, n):
                if i == 0:
                    wait_small_free(pe, SMALL0["CQ", g, 0] + 1)
                bank = small_job(n)
                wait_big_free(pe, BIG0["CE", g, i])
                for jj in range(4):
                    ins = mm(bank[32 * jj:32 * jj + 32, 0:S], vblk[:, 4 * i + jj, :], ptc[:, i % 2, jj, :])
                ins.then_inc(small_full[n % NS], 1)

            def queries_first(unit, src, full):
                blocks = src.shape[1]
                for t in range(GT):
                    for b in range(blocks):
                        at = (t * blocks + b) * P
                        ins = nc.tensor.transpose(unit[:, at:at + P], src[:, b, t * P:(t + 1) * P], ident[:, :])
                ins.then_inc(full, 1)

            def rows_by(n, lhsT, rhs, width=D):
                bank = small_job(n)
                for t in range(GT):
                    ins = mm(bank[:, t * width:(t + 1) * width], lhsT[:, t * P:(t + 1) * P], rhs)
                ins.then_inc(small_full[n % NS], 1)

            def up(g, e, n):
                if (g, e) == (0, 0):
                    pe.wait_ge(ld_w1, 16)
                    pe.wait_ge(ld_w2, 16)
                unit = big_job(n)
                for c in range(FC):
                    ins = mm(unit[:, c * S:(c + 1) * S], w1_sb[:, e, c * P:(c + 1) * P], x3T[:, g * S:(g + 1) * S])
                ins.then_inc(big_full[n % NB], 1)

            def down(g, e, n):
                bank = small_job(n)
                wait_big_free(pe, BIG0["MU", g, e])
                for t in range(GT):
                    for c in range(FC):
                        ins = mm(bank[:, t * D:(t + 1) * D], hid[:, e % 2, c, t * P:(t + 1) * P], w2_sb[:, e, c, :],
                                 start=(c == 0), stop=(c == FC - 1))
                ins.then_inc(small_full[n % NS], 1)

            for kind, g, i in ORDER:
                a = kind[0]
                n, m = SMALL0[kind, g, i], BIG0[kind, g, i]
                if kind == "FW":
                    fold()
                if kind == "KV":
                    keys_values(g, i, n)
                if kind == "LX":
                    if g == 0:
                        pe.wait_ge(consts_ready, 4)
                    pe.wait_ge(xn_ready, g + 1)
                    transposes(n, [xn[:, t, :] for t in range(GT)])
                if kind == "LS":
                    first_scores(g, i)
                if kind == "LT":
                    transpose_probs(g, i)
                if kind == "LV":
                    first_values(g, i)
                if kind == "SP":
                    if g == 0:
                        pe.wait_ge(ld_layer, 16 * 7)
                    wait_small_free(pe, SMALL0["LV", g, GT - 1])
                    transposes(n, tiles(g))
                if kind == "SQ":
                    self_projections(g, n)
                if kind == "SM":
                    self_max(g, i)
                if kind == "SX":
                    wait_big_free(pe, BIG0["SM", g, 5])
                    transposes(n, [negm["S"][:, t, :] for t in range(GT)], rows=H)
                if kind == "SE":
                    self_scores(g, i)
                if kind == "SV":
                    self_values(g, i, n)
                if kind == "SO":
                    wait_small_free(pe, SMALL0["SV", g, 3])
                    queries_first(big_job(m), oT["S"], big_full[m % NB])
                if kind == "ST":
                    wait_big_free(pe, BIG0["SO", g, 0])
                    transposes(n, [o_sb["S"][:, t, :] for t in range(GT)])
                if kind in ("SW", "CW"):
                    wait_small_free(pe, SMALL0[a + "T", g, 0])
                    rows_by(n, oTn[a], w_sb[a][:, 3, :])
                if kind == "CP":
                    pe.wait_ge(ln_ready["S"], g + 1)
                    transposes(n, tiles(g))
                if kind == "CQ":
                    cross_projections(g, n)
                if kind == "CM":
                    cross_max(g, i)
                if kind == "CX":
                    wait_big_free(pe, BIG0["CM", g, GT - 1])
                    transposes(n, [negm["C"][:, t, :] for t in range(GT)], rows=H)
                if kind == "CE":
                    cross_scores(g, i)
                if kind == "CV":
                    cross_values(g, i, n)
                if kind == "CO":
                    wait_small_free(pe, SMALL0["CV", g, 1])
                    queries_first(small_job(n), oT["C"], small_full[n % NS])
                if kind == "CT":
                    wait_small_free(pe, SMALL0["CO", g, 0])
                    transposes(n, [o_sb["C"][:, t, :] for t in range(GT)])
                if kind == "RX":
                    pe.wait_ge(ln_ready["C"], g + 1)
                    transposes(n, tiles(g))
                if kind == "RL":
                    wait_small_free(pe, SMALL0["RX", g, 0])
                    rows_by(n, x3T[:, g * S:(g + 1) * S], rw_sb[:, :], E)
                if kind == "RC":
                    pe.wait_ge(comb_ready, g + 1)
                    transposes(n, [comb[:, g * GT + t, :] for t in range(GT)], rows=E)
                if kind == "RB":
                    wait_small_free(pe, SMALL0["RC", g, 0])
                    rows_by(n, combT, b2_sb[:, :])
                if kind == "MU":
                    up(g, i, m)
                if kind == "MD":
                    down(g, i, n)


def kernel(**inputs):
    import concourse.bacc as bacc
    from concourse.bass_utils import run_bass_kernel_spmd

    a = {n.removeprefix("L1_xattn_"): np.asarray(v)
         for n, v in inputs.items()}
    rows = [a[n] for n in ("sa_bv", "sa_bo", "ca_bv", "ca_bo", "ln1_g", "ln1_b", "ln2_g", "ln2_b", "ln3_g",
                           "ln3_b", "router_b")] + [np.arange(E, dtype=np.float32)]
    arrays = {
        "x": a["x"].reshape(B * S, D),
        "ctx_t": a["ctx_1024"].reshape(B * SC, D).T,
        "wq_t": a["L0_xattn_wq"].T, "wk_t": a["L0_xattn_wk"].T, "wv_t": a["L0_xattn_wv"].T,
        "wo": a["L0_xattn_wo"],
        "norm_w": a["L0_xattn_norm_w"].reshape(D, 1),
        "sa_w": np.stack([a[n] for n in ("sa_wq", "sa_wk", "sa_wv", "sa_wo")]),
        "ca_w": np.stack([a[n] for n in ("ca_wq", "ca_wk", "ca_wv", "ca_wo")]),
        "bqk": np.stack([a[n] for n in ("sa_bq", "sa_bk", "ca_bq", "ca_bk")], axis=1),
        "rows": np.concatenate(rows).reshape(1, -1),
        "router_w": a["router_w"],
        "w1": a["e_w1"],
        "b1": a["e_b1"].reshape(E * FC, P).T,
        "w2": a["e_w2"], "b2": a["e_b2"],
    }
    arrays = {n: np.ascontiguousarray(v) for n, v in arrays.items()}
    nc = bacc.Bacc("TRN2", target_bir_lowering=False, num_devices=1)
    args = [nc.dram_tensor(n, v.shape, mybir.dt.from_np(v.dtype), kind="ExternalInput").ap() for n, v in arrays.items()]
    args.append(nc.dram_tensor("out", (B * S, D), F32, kind="ExternalOutput").ap())
    xattn_layer_kernel(nc, *args)
    r = run_bass_kernel_spmd(nc, [arrays], core_ids=[0])
    return r.results[0]["out"].reshape(B, S, D)
```

```python
from contextlib import ExitStack

import numpy as np
import concourse.bass as bass
from concourse import mybir

F32 = mybir.dt.float32
BF16 = mybir.dt.bfloat16
F32R = mybir.dt.float32r
U32 = mybir.dt.uint32
ALU = mybir.AluOpType
ACT = mybir.ActivationFunctionType
AX = mybir.AxisListType

P = 128
B, S, D = 8, 256, 128
SC = 64
H, DK, HD = 16, 64, 8
E, FF = 8, 512
FC = FF // P
NP = H // 2
G = B
GT = S // P
SLOTS = 6
Q_SLOTS = [(0, 1, 3), (1, 1, 2), (2, 1, 1)]
K_SLOTS = [(0, 3, 1), (0, 2, 1), (0, 1, 1)]
KR = SLOTS * 2 * HD
KM = KR + 4
NEG = -1.0e30
HIGH_BITS = 0xFFFFF000
RMS_EPS, LN_EPS = 1e-6, 1e-5
SCALE = float(HD) ** -0.5

NB, NS = 3, 2
BIG = {"KK": 1, "LS": 1, "LT": 1, "SM": 1, "SE": 2, "SO": 1, "CM": 1, "CE": 1, "MU": 1}
SMALL = {"FW": 8, "KV": 1, "LX": 1, "LV": 1, "SP": 1, "SQ": 2, "SX": 1, "SV": 1, "ST": 1, "SW": 1,
         "CP": 1, "CQ": 2, "CX": 1, "CV": 1, "CO": 1, "CT": 1, "CW": 1,
         "RX": 1, "RL": 1, "RC": 1, "RB": 1, "MD": 1}


TIMES = """
KK.0@0 KK.1@1742 LR@3316 LN@5687 KV.0@5838 KV.1@6773 LX@7267 LS.0@9060 LS.1@9425 LE.0@9580 LE.1@10053
LP.0@10894 LP.1@11965 LT.0@13828 LT.1@14449 LV.0@15417 LV.1@15843
SP@0 SQ@2883 SF@3161 SY@3874 SM.0@6405 SM.1@6595 SM.2@7175 SM.3@7179 SM.4@7364 SM.5@7635 SX@8346 SZ@9325
SE.0@10486 SE.1@11196 SV.0@11383 SE.2@11511 SV.1@11664 SE.3@12165 SV.2@12706 SV.3@12735 SO@13368 ST@14286
SW@14767 SN@16110
CP@0 CQ@179 CF@318 CY@1634 CM.0@3592 CM.1@4117 CX@4750 CZ@5877 CE.0@6888 CE.1@7784 CV.0@8522 CV.1@9507
CO@10496 CT@10994 CW@12201 CN@12990
RX@0 RL@189 RE@426 RT@1075 RG@1627 RD@1820 MU.0@1825 RC@2218 MU.1@2814 RB@3094 MD.0@3481 MU.2@4050 MD.1@4522
MU.3@5454 MD.2@5917 MU.4@6534 MD.3@6742 MU.5@7157 MD.4@7754 MU.6@8197 MD.5@8448 MU.7@9800 MD.6@10017
MD.7@10288 MN@12016 MO@14641
WS.0@0 WS.1@10 WS.2@20 WS.3@12074 WS.4@17816 WS.5@28929 WS.6@31439 WS.7@42463
"""
START = {"L": [3919, 9193, 14316, 20545, 25809, 31642, 36716, 46897],
         "S": [20085, 31315, 42486, 52383, 62448, 72397, 82527, 92527],
         "C": [39345, 49138, 58902, 68952, 78983, 89040, 98950, 108865],
         "M": [52933, 62753, 72813, 82869, 92954, 105241, 114875, 124498],
         "W": [0]}
PART = {"K": "L", "L": "L", "S": "S", "C": "C", "R": "M", "M": "M", "W": "W"}


def pipeline():
    timed = []
    for entry in TIMES.split():
        step, time = entry.split("@")
        kind, _, index = step.partition(".")
        for g, start in enumerate(START[PART[kind[0]]]):
            if kind != "KK" or g % 2 == 0:
                timed.append((start + int(time), len(timed), (kind, g, int(index or 0))))
    first = [("LR", 0, 0), ("FW", 0, 0)]
    return first + [step for _, _, step in sorted(timed) if step not in first]


ORDER = pipeline()


def first_jobs(count):
    at, out = 0, {}
    for step in ORDER:
        out[step] = at
        at += count.get(step[0], 0)
    return out


BIG0, SMALL0 = first_jobs(BIG), first_jobs(SMALL)


def xattn_layer_kernel(nc, x, ctx_t, wq_t, wk_t, wv_t, wo, norm_w, sa_w, ca_w, bqk, rows, router_w,
                       w1, b1, w2, b2, out):
    with ExitStack() as stack:
        def sb(name, shape, dt=F32):
            return stack.enter_context(nc.sbuf_tensor(name, shape, dt))

        def sem(name):
            return stack.enter_context(nc.semaphore(name))

        def both(make):
            return {"S": make("s"), "C": make("c")}

        CK = {"S": S, "C": SC}

        xs = sb("xs", [P, G * GT, D])
        ctxT = sb("ctxT", [P, B * SC])
        fold_w = sb("fold_w", [P, 4, NP, P])
        w2_sb = fold_w[:, :, :, :].rearrange("p a j n -> p (a j n)").rearrange("p (e c n) -> p e c n", e=E, c=FC)
        w1_high = sb("w1_high", [P, E, FF], F32R)
        w1_low = sb("w1_low", [P, E, FF], F32R)
        mF = sb("mF", [P, 2, NP, P])
        nF = sb("nF", [P, 2, NP, P])
        normw = sb("normw", [P, 1])
        kf = sb("kf", [P, 3, H * SC])
        vf = sb("vf", [P, 2, NP * P])
        xn = sb("xn", [P, GT, D])
        xnT = sb("xnT", [P, 2, S])
        pr = sb("pr", [P, 2, H * SC])
        prT = sb("prT", [P, 2, NP * P])
        wk_pad, wv_pad = (t[:, :, :].rearrange("p a (j n) -> p a j n", j=NP) for t in (pr, prT))
        hid = sb("hid", [P, 2, FC, S])
        w1_in = hid[:, :, :, :].rearrange("p a c n -> p (a c n)").rearrange("p (e f) -> p e f", e=E // 2)
        xT = both(lambda a: sb("xT_" + a, [P, S]))
        split32 = both(lambda a: sb("split32_" + a, [P, S + CK[a.upper()]]))
        parts = both(lambda a: sb("parts_" + a, [P, 3, S + CK[a.upper()]], BF16))
        qs = sb("qs", [P, NP, S], BF16)
        ks = sb("ks", [P, NP, 2, S], BF16)
        qc = sb("qc", [P, NP, S], BF16)
        kc = sb("kc", [P, NP, 2 * SC], BF16)
        negm = both(lambda a: sb("negm_" + a, [P, GT, H]))
        mparts = both(lambda a: sb("mparts_" + a, [H, 2, S], BF16))
        vaug = sb("vaug", [P, GT, H, 32])
        vblk = sb("vblk", [P, NP, 32])
        pt = sb("pt", [P, 4, 2, 3 * P])
        ptc = sb("ptc", [P, 2, 4, S])
        high_bits = sb("high_bits", [P, S])
        oT = {"S": sb("oT_s", [P, 4, S]), "C": sb("oT_c", [P, 2, S])}
        rsum = both(lambda a: sb("rsum_" + a, [P, GT * H]))
        o_sb = both(lambda a: sb("o_" + a, [P, GT, D]))
        oTn = both(lambda a: sb("oTn_" + a, [P, S]))
        w_sb = both(lambda a: sb("w_" + a, [P, 4, D]))
        bqk_sb = sb("bqk_sb", [P, 4])
        rows_sb = sb("rows_sb", [P, 10 * D + 2 * E])
        bc = rows_sb[:, 0:4 * D].rearrange("p (a d) -> p a d", a=4)
        lnr = rows_sb[:, 4 * D:10 * D].rearrange("p (a d) -> p a d", a=6)
        rb_sb = rows_sb[:, 10 * D:10 * D + E]
        iota = rows_sb[:, 10 * D + E:10 * D + 2 * E]
        rw_sb = sb("rw_sb", [P, E])
        b1_sb = sb("b1_sb", [P, E * FC])
        b2_sb = sb("b2_sb", [E, D])
        x3T = sb("x3T", [P, S])
        x_high = sb("x_high", [P, 2, S], F32R)
        x_low = sb("x_low", [P, 2, S], F32R)
        comb = sb("comb", [P, G * GT, E])
        combT = sb("combT", [E, S])
        ident = sb("ident", [P, P])
        identb = sb("identb", [P, P], BF16)
        mask_q = sb("mask_q", [P, P], BF16)
        mhalf = sb("mhalf", [P, 1])
        norms = ("L", "S", "C", "M")
        st = {a: sb("st_" + a, [P, GT, 6]) for a in norms}
        mv = {a: sb("mv_" + a, [P, GT, 2]) for a in norms}
        var = {a: sb("var_" + a, [P, GT]) for a in norms}
        rstd = {a: sb("rstd_" + a, [P, GT]) for a in norms}
        l0m = sb("l0m", [P, 2, H])
        l0s = sb("l0s", [P, 2, H])
        rt = sb("rt", [P, 6, GT, E])
        rs = sb("rs", [P, 6, GT])
        idx = sb("idx", [P, GT, E], U32)

        big = [stack.enter_context(nc.psum_tensor(f"big{i}", [P, 1024], F32)) for i in range(NB)]
        small = [stack.enter_context(nc.psum_tensor(f"small{i}", [P, 512], F32)) for i in range(NS)]

        q_d = both(lambda a: nc.dram_tensor("q_d_" + a, [G, P, SLOTS, S], BF16, kind="Internal").ap())
        k_d = {a: nc.dram_tensor("k_d_" + a, [G, P, SLOTS, n], BF16, kind="Internal").ap()
               for a, n in (("S", S), ("C", SC))}
        m_d = both(lambda a: nc.dram_tensor("m_d_" + a, [G, H, 2, S], BF16, kind="Internal").ap())

        big_full = [sem(f"big_full{i}") for i in range(NB)]
        big_free = [sem(f"big_free{i}") for i in range(NB)]
        small_full = [sem(f"small_full{i}") for i in range(NS)]
        small_free = [sem(f"small_free{i}") for i in range(NS)]
        ld_x, ld_ctx, ld_fold_k, ld_layer = sem("ld_x"), sem("ld_ctx"), sem("ld_fold_k"), sem("ld_layer")
        ld_x0, ld_fold_v, ld_w1, ld_w2 = sem("ld_x0"), sem("ld_fold_v"), sem("ld_w1"), sem("ld_w2")
        pads_ready = sem("pads_ready")
        w1_split = sem("w1_split")
        x_split = sem("x_split")
        consts_ready = sem("consts_ready")
        zeros_ready = sem("zeros_ready")
        bias_ready = sem("bias_ready")
        ones_ready = sem("ones_ready")
        dve_step = sem("dve_step")
        pool_step = sem("pool_step")
        var_ready = sem("var_ready")
        rstd_ready = sem("rstd_ready")
        xn_ready = sem("xn_ready")
        exp_ready = sem("exp_ready")
        rec_ready = sem("rec_ready")
        probs_ready = sem("probs_ready")
        parts_ready = both(lambda a: sem("parts_ready_" + a))
        parts_stored = both(lambda a: sem("parts_stored_" + a))
        stacked = both(lambda a: sem("stacked_" + a))
        m_stored = both(lambda a: sem("m_stored_" + a))
        m_rows = both(lambda a: sem("m_rows_" + a))
        ln_ready = both(lambda a: sem("ln_ready_" + a))
        logit_ready = sem("logit_ready")
        rexp_ready = sem("rexp_ready")
        masked = sem("masked")
        comb_ready = sem("comb_ready")
        res_ready = sem("res_ready")
        out_done = sem("out_done")

        def wait_big_full(eng, n):
            eng.wait_ge(big_full[n % NB], n // NB + 1)

        def wait_big_free(eng, n):
            if n >= 0:
                eng.wait_ge(big_free[n % NB], n // NB + 1)

        def wait_small_full(eng, n):
            eng.wait_ge(small_full[n % NS], n // NS + 1)

        def wait_small_free(eng, n):
            if n >= 0:
                eng.wait_ge(small_free[n % NS], n // NS + 1)

        STORED, STACKED = 16 * 6, 16 * 3

        def turn(*kinds):
            return {s: i for i, s in enumerate(s for s in ORDER if s[0] in kinds)}

        var_turn = turn("LR", "SW", "CW", "MN")

        block = stack.enter_context(nc.Block())

        @block.sync
        def _(sp):
            sp.dma_start(fold_w[:, 0], wq_t.rearrange("(j p) n -> p j n", p=P)).then_inc(ld_fold_k, 16)
            sp.dma_start(ctxT[:, :], ctx_t).then_inc(ld_ctx, 16)
            sp.dma_start(fold_w[:, 1], wo.rearrange("(j p) n -> p j n", p=P)).then_inc(ld_fold_v, 16)
            sp.dma_start(normw[:, :], norm_w).then_inc(ld_fold_v, 16)
            sp.dma_start(w_sb["S"][:, :, :], sa_w.rearrange("a d n -> d a n")).then_inc(ld_layer, 16)
            sp.dma_start(bqk_sb[:, :], bqk).then_inc(ld_layer, 16)
            sp.dma_start(rows_sb[:, :], rows.broadcast_to([P, 10 * D + 2 * E])).then_inc(ld_layer, 16)
            sp.dma_start(w_sb["C"][:, :, :], ca_w.rearrange("a d n -> d a n")).then_inc(ld_layer, 16)
            sp.dma_start(rw_sb[:, :], router_w).then_inc(ld_layer, 16)
            sp.dma_start(b1_sb[:, :], b1).then_inc(ld_layer, 16)
            sp.dma_start(b2_sb[:, :], b2).then_inc(ld_layer, 16)
            sp.dma_start(w1_in, w1[0:E // 2].rearrange("e d f -> d e f")).then_inc(ld_w1, 16)

            def store_parts(a, g):
                sp.wait_ge(parts_ready[a], g + 1)
                for dram, cols, slots in ((q_d[a], slice(0, S), Q_SLOTS), (k_d[a], slice(S, S + CK[a]), K_SLOTS)):
                    at = 0
                    for first, count, times in slots:
                        src = parts[a][:, first:first + count, cols]
                        if times > 1:
                            src = src.broadcast_to([P, times, S])
                        sp.dma_start(dram[g, :, at:at + count * times, :], src).then_inc(parts_stored[a], 16)
                        at += count * times

            def stack_parts(a, g):
                sp.wait_ge(parts_stored[a], STORED * (g + 1))
                if g > 0 and a == "S":
                    wait_big_full(sp, BIG0["SE", g - 1, 3] + 1)
                if g > 0 and a == "C":
                    wait_big_full(sp, BIG0["CE", g - 1, 1])
                q, k = (qs, ks) if a == "S" else (qc, kc.rearrange("p j (h t) -> p j h t", h=2))
                sp.dma_start(q[0:KR, :, :], q_d[a][g].rearrange("(j r) s t -> (r s) j t", j=NP)).then_inc(stacked[a], 16)
                for h2 in range(2):
                    src = k_d[a][g].rearrange("(j h d) s t -> h (d s) j t", j=NP, h=2)[h2]
                    sp.dma_start(k[KR // 2 * h2:KR // 2 * (h2 + 1), :, h2, :], src).then_inc(stacked[a], 16)

            def store_maxima(a, g):
                wait_small_free(sp, SMALL0[a + "X", g, 0])
                sp.dma_start(m_d[a][g], mparts[a][:, :, :]).then_inc(m_stored[a], 16)

            def maxima_rows(a, g):
                sp.wait_ge(m_stored[a], 16 * (g + 1))
                for part in range(2):
                    src = m_d[a][g, :, part, :].rearrange("(j h) t -> h j t", j=NP)
                    sp.dma_start((qs if a == "S" else qc)[KR + 2 * part:KR + 2 * part + 2, :, :], src).then_inc(
                        m_rows[a], 16)

            for kind, g, i in ORDER:
                if kind == "FW":
                    wait_small_full(sp, SMALL0["FW", 0, 0] + 7)
                    wait_small_full(sp, SMALL0["FW", 0, 0] + 6)
                    sp.dma_start(w2_sb, w2.rearrange("e (c p) n -> p e c n", p=P)).then_inc(ld_w2, 16)
                if (kind, i) == ("WS", E // 2 - 1):
                    sp.wait_ge(w1_split, E // 2)
                    sp.dma_start(w1_in, w1[E // 2:E].rearrange("e d f -> d e f")).then_inc(ld_w1, 16)
                if kind in ("SF", "CF"):
                    store_parts(kind[0], g)
                if kind in ("SY", "CY"):
                    stack_parts(kind[0], g)
                if kind in ("SX", "CX"):
                    store_maxima(kind[0], g)
                if kind in ("SZ", "CZ"):
                    maxima_rows(kind[0], g)
                if kind == "MO":
                    sp.wait_ge(res_ready, g + 1)
                    sp.dma_start(out.rearrange("(t p) d -> p t d", p=P)[:, g * GT:(g + 1) * GT],
                                 xs[:, g * GT:(g + 1) * GT, :]).then_inc(out_done, 16)
            sp.wait_ge(out_done, 16 * G)

        @block.gpsimd
        def _(pool):
            steps = [0]

            def step(ins):
                steps[0] += 1
                ins.then_inc(pool_step, 1)
                pool.wait_ge(pool_step, steps[0])

            def diagonal(m, pattern, multiplier, op, fill):
                step(nc.gpsimd.memset(m[:, :], 0.0))
                nc.gpsimd.affine_select(out=m[:, :], in_=m[:, :], compare_op=op, fill=fill, base=0,
                                        pattern=pattern, channel_multiplier=multiplier).then_inc(consts_ready, 1)

            diagonal(ident, [[-1, P]], 1, ALU.not_equal, 1.0)
            diagonal(identb, [[-1, P]], 1, ALU.not_equal, 1.0)
            diagonal(mask_q, [[-1, P]], 1, ALU.is_ge, NEG)

            def ones_rows(rows4, pattern):
                for base in (0, -2):
                    ins = nc.gpsimd.affine_select(out=rows4, in_=rows4, compare_op=ALU.not_equal, fill=1.0,
                                                  base=base, pattern=pattern, channel_multiplier=1)
                    if base == 0:
                        step(ins)
                ins.then_inc(ones_ready, 1)

            pool.wait_ge(zeros_ready, 1)
            pool.wait_ge(consts_ready, 3)
            ones_rows(ks[KR:KM, :, :, :], [[0, NP], [-1, 2], [0, S]])
            pool.wait_ge(ones_ready, 1)
            ones_rows(kc[KR:KM, :, :].rearrange("p j (h k) -> p j h k", h=2), [[0, NP], [-1, 2], [0, SC]])
            pool.wait_ge(ones_ready, 2)

            for kind, g, i in ORDER:
                m = BIG0[kind, g, i]
                if kind in ("LR", "SW", "CW", "MN"):
                    n = var_turn[kind, g, i]
                    pool.wait_ge(var_ready, n + 1)
                    nc.gpsimd.tensor_tensor(rstd[kind[0]][:, :], var[kind[0]][:, :],
                                            mhalf[:, :].broadcast_to([P, GT]), ALU.pow).then_inc(rstd_ready, 1)
                if kind == "SE":
                    for k in range(2):
                        wait_big_free(pool, m + k)
                        blocks = pt[:, (2 * i + k) % 4, :, 0:2 * P].rearrange("p h (b n) -> p h b n", b=2)
                        nc.gpsimd.affine_select(out=blocks, in_=blocks, compare_op=ALU.is_ge, fill=0.0, base=0,
                                                pattern=[[0, 2], [0, 2], [1, P]],
                                                channel_multiplier=-1).then_inc(masked, 1)
                if kind == "LP":
                    pool.wait_ge(rec_ready, GT * g + i + 1)
                    pv = pr[:, i % 2, :].rearrange("p (h k) -> p h k", h=H)
                    nc.gpsimd.tensor_tensor(pv, pv, l0s[:, i % 2, :].unsqueeze(2).broadcast_to([P, H, SC]),
                                            ALU.mult).then_inc(probs_ready, 1)

        @block.scalar
        def _(act):
            act.dma_start(xs[:, 0:GT, :], x[0:GT * P].rearrange("(t p) d -> p t d", p=P)).then_inc(ld_x0, 16)
            for pad, src, done in ((wk_pad, wk_t, ld_fold_k), (wv_pad, wv_t, ld_fold_v)):
                for h2 in range(2):
                    half = slice(DK * h2, DK * (h2 + 1))
                    act.dma_start(pad[half, h2], src.rearrange("(j p) n -> p j n", p=P)[half]).then_inc(done, 16)
            act.dma_start(xs[:, GT:, :], x[GT * P:].rearrange("(t p) d -> p t d", p=P)).then_inc(ld_x, 16)

            def copy_small(n, dst, width):
                wait_small_full(act, n)
                nc.scalar.copy(dst, small[n % NS][:, 0:width]).then_inc(small_free[n % NS], 1)

            for kind, g, i in ORDER:
                a = kind[0]
                n, m = SMALL0[kind, g, i], BIG0[kind, g, i]
                if kind == "FW":
                    for k in range(4):
                        copy_small(n + k, mF[:, k % 2, 4 * (k // 2):4 * (k // 2) + 4, :], 512)
                if kind == "KK":
                    wait_big_full(act, m)
                    for k in range(2):
                        ins = nc.scalar.activation(
                            kf[:, (g + k) % 3, :].rearrange("p (j h k) -> p h j k", j=NP, h=2)[:, i],
                            big[m % NB][:, :].rearrange("p (j b k) -> p b j k", j=NP, b=2)[:, k],
                            ACT.Copy, scale=normw[:, 0:1])
                    ins.then_inc(big_free[m % NB], 1)
                if kind == "LX":
                    copy_small(n, xnT[:, g % 2, :], S)
                if kind == "LE":
                    wait_big_free(act, BIG0["LS", g, i])
                    nc.scalar.activation(pr[:, i % 2, :], pr[:, i % 2, :], ACT.Exp).then_inc(exp_ready, 1)
                if kind == "LT":
                    wait_big_full(act, m)
                    nc.scalar.copy(prT[:, i % 2, :], big[m % NB][:, :]).then_inc(big_free[m % NB], 1)
                if kind in ("SP", "CP"):
                    copy_small(n, xT[a][:, :], S)
                if kind in ("SQ", "CQ"):
                    if g == 0:
                        act.wait_ge(bias_ready, 1)
                    else:
                        act.wait_ge(parts_ready[a], g)
                    c = 0 if a == "S" else 2
                    wait_small_full(act, n)
                    nc.scalar.activation(split32[a][:, 0:S], small[n % NS][:, 0:S], ACT.Identity,
                                         bias=bqk_sb[:, c:c + 1], scale=SCALE)
                    nc.scalar.activation(split32[a][:, S:S + CK[a]], small[n % NS][:, S:S + CK[a]], ACT.Identity,
                                         bias=bqk_sb[:, c + 1:c + 2]).then_inc(small_free[n % NS], 1)
                if kind == "SE":
                    for k in range(2):
                        wait_big_full(act, m + k)
                        nc.scalar.activation(pt[:, (2 * i + k) % 4, :, :],
                                             big[(m + k) % NB][:, :].rearrange("p (h n) -> p h n", h=2)[:, :, 0:3 * P],
                                             ACT.Exp).then_inc(big_free[(m + k) % NB], 1)
                if kind == "CE":
                    wait_big_full(act, m)
                    nc.scalar.activation(ptc[:, i % 2], big[m % NB][:, :].rearrange("p (j q) -> p j q", j=4),
                                         ACT.Exp).then_inc(big_free[m % NB], 1)
                if kind == "CV":
                    copy_small(n, oT["C"][:, i, :], S)
                if kind in ("ST", "CT"):
                    copy_small(n, oTn[a][:, :], S)
                if kind == "RX":
                    if g > 0:
                        act.wait_ge(x_split, g)
                    copy_small(n, x3T[:, :], S)
                if kind == "RE":
                    act.wait_ge(logit_ready, 2 * g + 1)
                    nc.scalar.activation(rt[:, 1, :, :], rt[:, 0, :, :], ACT.Exp).then_inc(rexp_ready, 1)
                if kind == "RG":
                    act.wait_ge(logit_ready, 2 * g + 2)
                    nc.scalar.activation(rs[:, 3, :], rs[:, 2, :], ACT.Exp).then_inc(rexp_ready, 1)
                if kind == "MU":
                    wait_big_full(act, m)
                    for c in range(FC):
                        ins = nc.scalar.activation(hid[:, i % 2, c, :], big[m % NB][:, c * S:(c + 1) * S],
                                                   ACT.Gelu, bias=b1_sb[:, i * FC + c:i * FC + c + 1])
                    ins.then_inc(big_free[m % NB], 1)

        @block.vector
        def _(dve):
            steps = [0]

            def step(ins):
                steps[0] += 1
                ins.then_inc(dve_step, 1)
                dve.wait_ge(dve_step, steps[0])

            def padding():
                for pad in (wk_pad, wv_pad):
                    nc.vector.memset(pad[DK:P, 0], 0.0)
                    nc.vector.memset(pad[0:DK, 1], 0.0).then_inc(pads_ready, 1)
                nc.vector.memset(ks[:, :, :, :].bitcast(U32), 0)
                nc.vector.memset(kc[:, :, :].bitcast(U32), 0)
                nc.vector.memset(mhalf[:, :], -0.5).then_inc(zeros_ready, 1)
                nc.vector.memset(vaug[:, :, :, :], 0.0)
                step(nc.vector.memset(vblk[:, :, :], 0.0))
                nc.vector.memset(vaug[:, :, :, HD:HD + 1], 1.0)
                nc.vector.memset(vblk[0:SC, :, HD:HD + 1], 1.0)
                nc.vector.memset(vblk[SC:P, :, 16 + HD:16 + HD + 1], 1.0)

            def fold():
                for i in range(4):
                    n = SMALL0["FW", 0, 0] + 4 + i
                    wait_small_full(dve, n)
                    nc.vector.tensor_copy(nF[:, i % 2, 4 * (i // 2):4 * (i // 2) + 4, :],
                                          small[n % NS][:, :]).then_inc(small_free[n % NS], 1)
                dve.wait_ge(ld_layer, 16 * 7)
                q_bias = bqk_sb[:, :].rearrange("p (a b) -> p a b", a=2)[:, :, 0]
                nc.vector.tensor_scalar(q_bias, q_bias, SCALE, None, ALU.mult).then_inc(bias_ready, 1)

            def group(g):
                return xs[:, g * GT:(g + 1) * GT, :]

            def copy_small(n, dst, width):
                wait_small_full(dve, n)
                nc.vector.tensor_copy(dst, small[n % NS][:, 0:width]).then_inc(small_free[n % NS], 1)

            def rms(g):
                if g == 0:
                    dve.wait_ge(ld_x0, 16)
                else:
                    dve.wait_ge(ld_x, 16)
                    wait_small_full(dve, SMALL0["LX", g - 1, 0])
                step(nc.vector.tensor_tensor(xn[:, :, :], group(g), group(g), ALU.mult))
                step(nc.vector.reduce_sum(var["L"][:, :], xn[:, :, :], AX.X))
                nc.vector.tensor_scalar(var["L"][:, :], var["L"][:, :], 1.0 / D, RMS_EPS, ALU.mult,
                                        ALU.add).then_inc(var_ready, 1)

            def normed(g):
                dve.wait_ge(rstd_ready, var_turn["LR", g, 0] + 1)
                nc.vector.tensor_tensor(xn[:, :, :], group(g), rstd["L"][:, :].unsqueeze(2).broadcast_to([P, GT, D]),
                                        ALU.mult).then_inc(xn_ready, 1)

            def scores(g, t):
                n = BIG0["LS", g, t]
                wait_big_full(dve, n)
                s = big[n % NB][:, :].rearrange("p (h k) -> p h k", h=H)
                step(nc.vector.reduce_max(l0m[:, t % 2, :], s, AX.X, negate=True))
                nc.vector.tensor_tensor(pr[:, t % 2, :].rearrange("p (h k) -> p h k", h=H), s,
                                        l0m[:, t % 2, :].unsqueeze(2).broadcast_to([P, H, SC]),
                                        ALU.add).then_inc(big_free[n % NB], 1)

            def sums(g, t):
                dve.wait_ge(exp_ready, GT * g + t + 1)
                step(nc.vector.reduce_sum(l0s[:, t % 2, :], pr[:, t % 2, :].rearrange("p (h k) -> p h k", h=H), AX.X))
                nc.vector.reciprocal(l0s[:, t % 2, :], l0s[:, t % 2, :]).then_inc(rec_ready, 1)

            def first_residual(g, t):
                n = SMALL0["LV", g, t]
                wait_small_full(dve, n)
                nc.vector.tensor_tensor(xs[:, g * GT + t, :], xs[:, g * GT + t, :], small[n % NS][:, 0:D],
                                        ALU.add).then_inc(small_free[n % NS], 1)

            def split(a, g):
                width = S + CK[a]
                n = SMALL0[a + "Q", g, 0]
                q = split32[a][:, 0:width]
                part = [parts[a][:, i, 0:width] for i in range(NB)]
                wait_small_free(dve, n)
                if g > 0:
                    dve.wait_ge(parts_stored[a], 16 * g)
                step(nc.vector.tensor_copy(part[0], q))
                step(nc.vector.tensor_tensor(q, q, part[0], ALU.subtract))
                step(nc.vector.tensor_copy(part[1], q))
                nc.vector.tensor_tensor(part[2], q, part[1], ALU.subtract).then_inc(parts_ready[a], 1)

            def self_values(g):
                n = SMALL0["SQ", g, 0] + 1
                wait_small_full(dve, n)
                for t in range(GT):
                    ins = nc.vector.tensor_tensor(vaug[:, t, :, 0:HD],
                                                  small[n % NS][:, t * D:(t + 1) * D].rearrange("p (h d) -> p h d", h=H),
                                                  bc[:, 0, :].rearrange("p (h d) -> p h d", h=H), ALU.add)
                ins.then_inc(small_free[n % NS], 1)

            def cross_values(g):
                n = SMALL0["CQ", g, 0] + 1
                wait_small_full(dve, n)
                for h2 in range(2):
                    half = slice(h2 * SC, (h2 + 1) * SC)
                    ins = nc.vector.tensor_tensor(
                        vblk[half, :, 16 * h2:16 * h2 + HD],
                        small[n % NS][half, 0:64].rearrange("p (j d) -> p j d", j=NP),
                        bc[half, 2, :].rearrange("p (j h d) -> p h j d", j=NP, h=2)[:, h2], ALU.add)
                ins.then_inc(small_free[n % NS], 1)

            def maximum(n, dst, keys):
                wait_big_full(dve, n)
                nc.vector.reduce_max(dst, big[n % NB][:, :].rearrange("p (h k) -> p h k", k=keys), AX.X,
                                     negate=True).then_inc(big_free[n % NB], 1)

            def max_parts(a, g):
                n = SMALL0[a + "X", g, 0]
                wait_small_full(dve, n)
                if g > 0:
                    dve.wait_ge(m_stored[a], 16 * g)
                step(nc.vector.tensor_copy(mparts[a][:, 0, :], small[n % NS][0:H, 0:S]))
                nc.vector.tensor_tensor(mparts[a][:, 1, :], small[n % NS][0:H, 0:S], mparts[a][:, 0, :],
                                        ALU.subtract).then_inc(small_free[n % NS], 1)

            def divide(a, g, psum, free, stride):
                o = psum.rearrange("p (h c) -> p h c", c=stride)
                step(nc.vector.reciprocal(rsum[a][:, :], o[:, :, HD]))
                nc.vector.tensor_tensor(o_sb[a][:, :, :].rearrange("p t (h d) -> p (t h) d", h=H), o[:, :, 0:HD],
                                        rsum[a][:, :].unsqueeze(2).broadcast_to([P, GT * H, HD]),
                                        ALU.mult).then_inc(free, 1)

            def norm_statistics(a, g):
                for t in range(GT):
                    ins = nc.vector.bn_stats(st[a][:, t, :], xs[:, g * GT + t, :])
                step(ins)
                for t in range(GT):
                    ins = nc.vector.bn_aggr(mv[a][:, t, :], st[a][:, t, :])
                step(ins)
                nc.vector.tensor_scalar(var[a][:, :], mv[a][:, :, 1], LN_EPS, None, ALU.add).then_inc(var_ready, 1)

            def residual(a, g):
                n = SMALL0[a + "W", g, 0]
                wait_small_full(dve, n)
                nc.vector.tensor_tensor(group(g), group(g), small[n % NS][:, 0:S].rearrange("p (t d) -> p t d", t=GT),
                                        ALU.add).then_inc(small_free[n % NS], 1)
                wait_small_free(dve, n)
                bo = bc[:, 1 if a == "S" else 3, :]
                step(nc.vector.tensor_tensor(group(g), group(g), bo.unsqueeze(1).broadcast_to([P, GT, D]), ALU.add))
                norm_statistics(a, g)

            def layernorm(a, g, kind, which, done):
                dve.wait_ge(rstd_ready, var_turn[kind, g, 0] + 1)
                for t in range(GT):
                    ins = nc.vector.tensor_scalar(xs[:, g * GT + t, :], xs[:, g * GT + t, :], mv[a][:, t, 0:1],
                                                  rstd[a][:, t:t + 1], ALU.subtract, ALU.mult)
                step(ins)
                gain, shift = (lnr[:, 2 * which + i, :].unsqueeze(1).broadcast_to([P, GT, D]) for i in range(2))
                step(nc.vector.tensor_tensor(group(g), group(g), gain, ALU.mult))
                nc.vector.tensor_tensor(group(g), group(g), shift, ALU.add).then_inc(done, 1)

            def col(ap):
                return ap.unsqueeze(2).broadcast_to([P, GT, E])

            def row(ap):
                return ap.unsqueeze(1).broadcast_to([P, GT, E])

            logits, prob, eq1, eq2, m8, idf = (rt[:, k] for k in range(6))
            neg, inv, dif, e2, w_1, w_2 = (rs[:, k, :] for k in range(6))

            def router_logits(g):
                n = SMALL0["RL", g, 0]
                wait_small_full(dve, n)
                nc.vector.tensor_tensor(logits, small[n % NS][:, 0:GT * E].rearrange("p (t e) -> p t e", t=GT),
                                        row(rb_sb), ALU.add).then_inc(small_free[n % NS], 1)
                wait_small_free(dve, n)
                step(nc.vector.reduce_max(neg, logits, AX.X, negate=True))
                nc.vector.tensor_tensor(logits, logits, col(neg), ALU.add).then_inc(logit_ready, 1)

            def router_top2(g):
                dve.wait_ge(rexp_ready, 2 * g + 1)
                step(nc.vector.reduce_sum(inv, prob, AX.X))
                step(nc.vector.reciprocal(inv, inv))
                step(nc.vector.tensor_tensor(prob, prob, col(inv), ALU.mult))
                for t in range(GT):
                    ins = nc.vector.max(m8[:, t, :], prob[:, t, :])
                step(ins)
                nc.vector.tensor_tensor(dif, m8[:, :, 1], m8[:, :, 0], ALU.subtract).then_inc(logit_ready, 1)
                for t in range(GT):
                    ins = nc.vector.max_index(idx[:, t, :], m8[:, t, :], prob[:, t, :])
                step(ins)
                step(nc.vector.tensor_copy(idf, idx[:, :, :]))

            def router_combine(g):
                dve.wait_ge(rexp_ready, 2 * g + 2)
                nc.vector.tensor_tensor(eq1, row(iota), col(idf[:, :, 0]), ALU.is_equal)
                nc.vector.tensor_tensor(eq2, row(iota), col(idf[:, :, 1]), ALU.is_equal)
                step(nc.vector.tensor_scalar(w_1, e2, 1.0, None, ALU.add))
                step(nc.vector.reciprocal(w_1, w_1))
                step(nc.vector.tensor_tensor(w_2, e2, w_1, ALU.mult))
                nc.vector.tensor_tensor(eq1, eq1, col(w_1), ALU.mult)
                step(nc.vector.tensor_tensor(eq2, eq2, col(w_2), ALU.mult))
                nc.vector.tensor_tensor(comb[:, g * GT:(g + 1) * GT, :], eq1, eq2, ALU.add).then_inc(comb_ready, 1)

            def expert_bias(g):
                n = SMALL0["RB", g, 0]
                wait_small_full(dve, n)
                nc.vector.tensor_tensor(group(g), group(g), small[n % NS][:, 0:S].rearrange("p (t d) -> p t d", t=GT),
                                        ALU.add).then_inc(small_free[n % NS], 1)

            def expert(g, e):
                n = SMALL0["MD", g, e]
                wait_small_full(dve, n)
                wait_small_free(dve, SMALL0["MD", g, e - 1] if e > 0 else SMALL0["RB", g, 0])
                for t in range(GT):
                    ins = nc.vector.scalar_tensor_tensor(
                        xs[:, g * GT + t, :], small[n % NS][:, t * D:(t + 1) * D], comb[:, g * GT + t, e:e + 1],
                        xs[:, g * GT + t, :], ALU.mult, ALU.add)
                ins.then_inc(small_free[n % NS], 1)

            padding()

            def split_high_low(x, high, low, done):
                cols = x.shape[1]
                for at in range(0, cols, S):
                    part = slice(at, at + S)
                    step(nc.vector.tensor_scalar(high_bits[:, :].bitcast(U32), x[:, part].bitcast(U32), HIGH_BITS, None,
                                                 ALU.bitwise_and))
                    step(nc.vector.tensor_copy(high[:, part], high_bits[:, :]))
                    last = nc.vector.tensor_tensor(low[:, part], x[:, part], high_bits[:, :], ALU.subtract)
                    if at + S < cols:
                        step(last)
                last.then_inc(done, 1)
                dve.wait_ge(done, g + 1 if done is x_split else i + 1)

            for kind, g, i in ORDER:
                a = kind[0]
                n, m = SMALL0[kind, g, i], BIG0[kind, g, i]
                if kind == "FW":
                    fold()
                if kind == "WS":
                    dve.wait_ge(ld_w1, 16 * (2 * i // E + 1))
                    split_high_low(w1_in[:, i % (E // 2), :], w1_high[:, i, :], w1_low[:, i, :], w1_split)
                if kind == "RX":
                    wait_small_free(dve, n)
                    split_high_low(x3T[:, :], x_high[:, g % 2, :], x_low[:, g % 2, :], x_split)
                if kind == "KV":
                    copy_small(n, vf[:, g % 2, i * 512:(i + 1) * 512], 512)
                if kind == "LR":
                    rms(g)
                if kind == "LN":
                    normed(g)
                if kind == "LS":
                    scores(g, i)
                if kind == "LP":
                    sums(g, i)
                if kind == "LV":
                    first_residual(g, i)
                if kind == "SQ":
                    self_values(g)
                if kind == "CQ":
                    cross_values(g)
                if kind in ("SF", "CF"):
                    split(a, g)
                if kind == "SM":
                    maximum(m, negm["S"][:, 0, 8 * i:8 * i + 8] if i < 2 else negm["S"][:, 1, 4 * (i - 2):4 * (i - 1)],
                            P if i < 2 else 2 * P)
                if kind == "CM":
                    maximum(m, negm["C"][:, i, :], SC)
                if kind in ("SX", "CX"):
                    max_parts(a, g)
                if kind == "SV":
                    copy_small(n, oT["S"][:, i, :], S)
                if kind == "SO":
                    wait_big_full(dve, m)
                    divide("S", g, big[m % NB][:, :], big_free[m % NB], 32)
                if kind == "CO":
                    wait_small_full(dve, n)
                    divide("C", g, small[n % NS][:, :], small_free[n % NS], 16)
                if kind in ("SW", "CW"):
                    residual(a, g)
                if kind == "SN":
                    layernorm("S", g, "SW", 0, ln_ready["S"])
                if kind == "CN":
                    layernorm("C", g, "CW", 1, ln_ready["C"])
                if kind == "RL":
                    router_logits(g)
                if kind == "RT":
                    router_top2(g)
                if kind == "RD":
                    router_combine(g)
                if kind == "RC":
                    wait_small_full(dve, n)
                    nc.vector.tensor_copy(combT[:, :], small[n % NS][0:E, 0:S]).then_inc(small_free[n % NS], 1)
                if kind == "RB":
                    expert_bias(g)
                if kind == "MD":
                    expert(g, i)
                if kind == "MN":
                    wait_small_free(dve, SMALL0["MD", g, E - 1])
                    norm_statistics("M", g)
                if kind == "MO":
                    layernorm("M", g, "MN", 2, res_ready)

        @block.tensor
        def _(pe):
            def mm(out_, lhsT, rhs, start=True, stop=True):
                return nc.tensor.matmul(out_, lhsT, rhs, start=start, stop=stop)

            def small_job(n):
                wait_small_free(pe, n - NS)
                return small[n % NS]

            def big_job(n):
                wait_big_free(pe, n - NB)
                return big[n % NB]

            def fold():
                for i in range(8):
                    n = SMALL0["FW", 0, 0] + i
                    if i == 0:
                        pe.wait_ge(ld_fold_k, 16 * 3)
                        pe.wait_ge(pads_ready, 1)
                    if i == 4:
                        pe.wait_ge(ld_fold_v, 16 * 4)
                        pe.wait_ge(pads_ready, 2)
                    bank = small_job(n)
                    h2, j0 = i % 2, 4 * (i % 4 // 2)
                    pad, other = (wk_pad, 0) if i < 4 else (wv_pad, 1)
                    for jj in range(4):
                        ins = mm(bank[:, jj * P:(jj + 1) * P], pad[:, h2, j0 + jj, :], fold_w[:, other, j0 + jj, :])
                    ins.then_inc(small_full[n % NS], 1)
                pe.wait_ge(ld_ctx, 16)
                wait_small_free(pe, SMALL0["FW", 0, 0] + 3)
                wait_small_free(pe, SMALL0["FW", 0, 0] + 7)

            def first_keys(g, i, n):
                unit = big_job(n)
                for j in range(NP):
                    ins = mm(unit[:, j * 2 * SC:(j + 1) * 2 * SC], mF[:, i, j, :], ctxT[:, g * SC:(g + 2) * SC])
                ins.then_inc(big_full[n % NB], 1)

            def first_vals(g, i, n):
                bank = small_job(n)
                for h2 in range(2):
                    ins = mm(bank[64 * h2:64 * h2 + 64, :], ctxT[:, g * SC:(g + 1) * SC], nF[:, h2, 4 * i:4 * i + 4, :])
                ins.then_inc(small_full[n % NS], 1)

            def transposes(n, sources, rows=P):
                bank = small_job(n)
                for t, src in enumerate(sources):
                    ins = nc.tensor.transpose(bank[0:rows, t * P:(t + 1) * P], src, ident[:, :])
                ins.then_inc(small_full[n % NS], 1)

            def tiles(g):
                return [xs[:, g * GT + t, :] for t in range(GT)]

            def first_scores(g, t):
                if t == 0:
                    wait_small_free(pe, SMALL0["LX", g, 0])
                    wait_big_free(pe, BIG0["KK", g - g % 2, 1])
                    wait_small_free(pe, SMALL0["KV", g, 0])
                    wait_small_free(pe, SMALL0["KV", g, 1])
                n = BIG0["LS", g, t]
                unit = big_job(n)
                for i in range(2):
                    ins = mm(unit[:, i * 512:(i + 1) * 512], xnT[:, g % 2, t * P:(t + 1) * P],
                             kf[:, g % 3, i * 512:(i + 1) * 512])
                ins.then_inc(big_full[n % NB], 1)

            def transpose_probs(g, t):
                n = BIG0["LT", g, t]
                unit = big_job(n)
                pe.wait_ge(probs_ready, GT * g + t + 1)
                for j in range(NP):
                    ins = nc.tensor.transpose(unit[:, j * P:(j + 1) * P], pr[:, t % 2, j * P:(j + 1) * P], ident[:, :])
                ins.then_inc(big_full[n % NB], 1)

            def first_values(g, t):
                n = SMALL0["LV", g, t]
                bank = small_job(n)
                wait_big_free(pe, BIG0["LT", g, t])
                for j in range(NP):
                    ins = mm(bank[:, 0:D], prT[:, t % 2, j * P:(j + 1) * P], vf[:, g % 2, j * P:(j + 1) * P],
                             start=(j == 0), stop=(j == NP - 1))
                ins.then_inc(small_full[n % NS], 1)

            def self_projections(g, n):
                wait_small_free(pe, SMALL0["SP", g, 0])
                bank = small_job(n)
                for i in range(2):
                    ins = mm(bank[:, i * S:(i + 1) * S], w_sb["S"][:, i, :], xT["S"][:, :])
                ins.then_inc(small_full[n % NS], 1)
                n += 1
                bank = small_job(n)
                for t in range(GT):
                    ins = mm(bank[:, t * D:(t + 1) * D], xT["S"][:, t * P:(t + 1) * P], w_sb["S"][:, 2, :])
                ins.then_inc(small_full[n % NS], 1)

            def cross_projections(g, n):
                wait_small_free(pe, SMALL0["CP", g, 0])
                ctx = ctxT[:, g * SC:(g + 1) * SC]
                bank = small_job(n)
                mm(bank[:, 0:S], w_sb["C"][:, 0, :], xT["C"][:, :])
                mm(bank[:, S:S + SC], w_sb["C"][:, 1, :], ctx).then_inc(small_full[n % NS], 1)
                n += 1
                bank = small_job(n)
                for h2 in range(2):
                    ins = mm(bank[64 * h2:64 * h2 + 64, 0:64], ctx,
                             w_sb["C"][:, 2, :].rearrange("p (j h d) -> p h j d", j=NP, h=2)[:, h2])
                ins.then_inc(small_full[n % NS], 1)

            def self_max(g, i):
                if i == 0:
                    pe.wait_ge(stacked["S"], STACKED * (g + 1))
                    if g == 0:
                        pe.wait_ge(ones_ready, 2)
                n = BIG0["SM", g, i]
                unit = big_job(n)
                t = 0 if i < 2 else 1
                keys, pairs = P * (t + 1), 4 // (t + 1)
                for jj in range(pairs):
                    j = jj + pairs * (i if i < 2 else i - 2)
                    reg = unit[:, jj * 2 * keys:(jj + 1) * 2 * keys].rearrange("p (h k) -> p h k", h=2)
                    mm(reg, qs[0:KR, j, t * P:(t + 1) * P], ks[0:KR, j, :, 0:keys], stop=False)
                    ins = mm(reg[:, :, keys - P:keys], identb[:, :],
                             mask_q[:, :].unsqueeze(1).broadcast_to([P, 2, P]), start=False)
                ins.then_inc(big_full[n % NB], 1)

            def cross_max(g, t):
                if t == 0:
                    pe.wait_ge(stacked["C"], STACKED * (g + 1))
                n = BIG0["CM", g, t]
                unit = big_job(n)
                for j in range(NP):
                    ins = mm(unit[:, j * P:(j + 1) * P], qc[0:KR, j, t * P:(t + 1) * P], kc[0:KR, j, :])
                ins.then_inc(big_full[n % NB], 1)

            def self_scores(g, i):
                if i == 0:
                    pe.wait_ge(m_rows["S"], 32 * (g + 1))
                for j in (2 * i, 2 * i + 1):
                    n = BIG0["SE", g, i] + j - 2 * i
                    unit = big_job(n)
                    for h2 in range(2):
                        reg = unit[:, 512 * h2:512 * (h2 + 1)]
                        mm(reg[:, P:3 * P], ks[0:KM, j, h2, 0:P], qs[0:KM, j, 0:S])
                        ins = mm(reg[:, 0:P], ks[0:KM, j, h2, P:S], qs[0:KM, j, P:S])
                    ins.then_inc(big_full[n % NB], 1)

            def self_values(g, i, n):
                if i == 0:
                    wait_small_free(pe, SMALL0["SQ", g, 0] + 1)
                bank = small_job(n)
                pe.wait_ge(masked, NP * g + 2 * i + 2)
                for kt in range(2):
                    for hh in range(4):
                        e = pt[:, (2 * i + hh // 2) % 4, hh % 2, :]
                        ins = mm(bank[32 * hh:32 * hh + 32, kt * P:S], vaug[:, kt, 4 * i + hh, :],
                                 e[:, 0:P] if kt else e[:, P:3 * P], start=(kt == 0), stop=(kt == 1))
                ins.then_inc(small_full[n % NS], 1)

            def cross_scores(g, i):
                if i == 0:
                    pe.wait_ge(m_rows["C"], 32 * (g + 1))
                n = BIG0["CE", g, i]
                unit = big_job(n)
                for jj in range(4):
                    ins = mm(unit[:, jj * S:(jj + 1) * S], kc[0:KM, 4 * i + jj, :], qc[0:KM, 4 * i + jj, :])
                ins.then_inc(big_full[n % NB], 1)

            def cross_values(g, i, n):
                if i == 0:
                    wait_small_free(pe, SMALL0["CQ", g, 0] + 1)
                bank = small_job(n)
                wait_big_free(pe, BIG0["CE", g, i])
                for jj in range(4):
                    ins = mm(bank[32 * jj:32 * jj + 32, 0:S], vblk[:, 4 * i + jj, :], ptc[:, i % 2, jj, :])
                ins.then_inc(small_full[n % NS], 1)

            def queries_first(unit, src, full):
                blocks = src.shape[1]
                for t in range(GT):
                    for b in range(blocks):
                        at = (t * blocks + b) * P
                        ins = nc.tensor.transpose(unit[:, at:at + P], src[:, b, t * P:(t + 1) * P], ident[:, :])
                ins.then_inc(full, 1)

            def rows_by(n, lhsT, rhs, width=D):
                bank = small_job(n)
                for t in range(GT):
                    ins = mm(bank[:, t * width:(t + 1) * width], lhsT[:, t * P:(t + 1) * P], rhs)
                ins.then_inc(small_full[n % NS], 1)

            def up(g, e, n):
                if (g, e) == (0, 0):
                    pe.wait_ge(w1_split, E)
                    pe.wait_ge(ld_w2, 16)
                if e == 0:
                    pe.wait_ge(x_split, g + 1)
                unit = big_job(n)
                for c in range(FC):
                    part = slice(c * P, (c + 1) * P)
                    out_ = unit[:, c * S:(c + 1) * S]
                    mm(out_, w1_high[:, e, part], x_high[:, g % 2, :], stop=False)
                    mm(out_, w1_high[:, e, part], x_low[:, g % 2, :], start=False, stop=False)
                    ins = mm(out_, w1_low[:, e, part], x_high[:, g % 2, :], start=False)
                ins.then_inc(big_full[n % NB], 1)

            def down(g, e, n):
                bank = small_job(n)
                wait_big_free(pe, BIG0["MU", g, e])
                for t in range(GT):
                    for c in range(FC):
                        ins = mm(bank[:, t * D:(t + 1) * D], hid[:, e % 2, c, t * P:(t + 1) * P], w2_sb[:, e, c, :],
                                 start=(c == 0), stop=(c == FC - 1))
                ins.then_inc(small_full[n % NS], 1)

            for kind, g, i in ORDER:
                a = kind[0]
                n, m = SMALL0[kind, g, i], BIG0[kind, g, i]
                if kind == "FW":
                    fold()
                if kind == "KV":
                    first_vals(g, i, n)
                if kind == "KK":
                    first_keys(g, i, m)
                if kind == "LX":
                    if g == 0:
                        pe.wait_ge(consts_ready, 3)
                    pe.wait_ge(xn_ready, g + 1)
                    transposes(n, [xn[:, t, :] for t in range(GT)])
                if kind == "LS":
                    first_scores(g, i)
                if kind == "LT":
                    transpose_probs(g, i)
                if kind == "LV":
                    first_values(g, i)
                if kind == "SP":
                    if g == 0:
                        pe.wait_ge(ld_layer, 16 * 7)
                    wait_small_free(pe, SMALL0["LV", g, GT - 1])
                    transposes(n, tiles(g))
                if kind == "SQ":
                    self_projections(g, n)
                if kind == "SM":
                    self_max(g, i)
                if kind == "SX":
                    wait_big_free(pe, BIG0["SM", g, 5])
                    transposes(n, [negm["S"][:, t, :] for t in range(GT)], rows=H)
                if kind == "SE":
                    self_scores(g, i)
                if kind == "SV":
                    self_values(g, i, n)
                if kind == "SO":
                    wait_small_free(pe, SMALL0["SV", g, 3])
                    queries_first(big_job(m), oT["S"], big_full[m % NB])
                if kind == "ST":
                    wait_big_free(pe, BIG0["SO", g, 0])
                    transposes(n, [o_sb["S"][:, t, :] for t in range(GT)])
                if kind in ("SW", "CW"):
                    wait_small_free(pe, SMALL0[a + "T", g, 0])
                    rows_by(n, oTn[a], w_sb[a][:, 3, :])
                if kind == "CP":
                    pe.wait_ge(ln_ready["S"], g + 1)
                    transposes(n, tiles(g))
                if kind == "CQ":
                    cross_projections(g, n)
                if kind == "CM":
                    cross_max(g, i)
                if kind == "CX":
                    wait_big_free(pe, BIG0["CM", g, GT - 1])
                    transposes(n, [negm["C"][:, t, :] for t in range(GT)], rows=H)
                if kind == "CE":
                    cross_scores(g, i)
                if kind == "CV":
                    cross_values(g, i, n)
                if kind == "CO":
                    wait_small_free(pe, SMALL0["CV", g, 1])
                    queries_first(small_job(n), oT["C"], small_full[n % NS])
                if kind == "CT":
                    wait_small_free(pe, SMALL0["CO", g, 0])
                    transposes(n, [o_sb["C"][:, t, :] for t in range(GT)])
                if kind == "RX":
                    pe.wait_ge(ln_ready["C"], g + 1)
                    transposes(n, tiles(g))
                if kind == "RL":
                    wait_small_free(pe, SMALL0["RX", g, 0])
                    rows_by(n, x3T[:, :], rw_sb[:, :], E)
                if kind == "RC":
                    pe.wait_ge(comb_ready, g + 1)
                    transposes(n, [comb[:, g * GT + t, :] for t in range(GT)], rows=E)
                if kind == "RB":
                    wait_small_free(pe, SMALL0["RC", g, 0])
                    rows_by(n, combT, b2_sb[:, :])
                if kind == "MU":
                    up(g, i, m)
                if kind == "MD":
                    down(g, i, n)


def kernel(**inputs):
    import concourse.bacc as bacc
    from concourse.bass_utils import run_bass_kernel_spmd

    a = {n.removeprefix("L1_xattn_"): np.asarray(v)
         for n, v in inputs.items()}
    rows = [a[n] for n in ("sa_bv", "sa_bo", "ca_bv", "ca_bo", "ln1_g", "ln1_b", "ln2_g", "ln2_b", "ln3_g",
                           "ln3_b", "router_b")] + [np.arange(E, dtype=np.float32)]
    arrays = {
        "x": a["x"].reshape(B * S, D),
        "ctx_t": a["ctx_1024"].reshape(B * SC, D).T,
        "wq_t": a["L0_xattn_wq"].T, "wk_t": a["L0_xattn_wk"].T, "wv_t": a["L0_xattn_wv"].T,
        "wo": a["L0_xattn_wo"],
        "norm_w": a["L0_xattn_norm_w"].reshape(D, 1),
        "sa_w": np.stack([a[n] for n in ("sa_wq", "sa_wk", "sa_wv", "sa_wo")]),
        "ca_w": np.stack([a[n] for n in ("ca_wq", "ca_wk", "ca_wv", "ca_wo")]),
        "bqk": np.stack([a[n] for n in ("sa_bq", "sa_bk", "ca_bq", "ca_bk")], axis=1),
        "rows": np.concatenate(rows).reshape(1, -1),
        "router_w": a["router_w"],
        "w1": a["e_w1"],
        "b1": a["e_b1"].reshape(E * FC, P).T,
        "w2": a["e_w2"], "b2": a["e_b2"],
    }
    arrays = {n: np.ascontiguousarray(v) for n, v in arrays.items()}
    nc = bacc.Bacc("TRN2", target_bir_lowering=False, num_devices=1)
    args = [nc.dram_tensor(n, v.shape, mybir.dt.from_np(v.dtype), kind="ExternalInput").ap() for n, v in arrays.items()]
    args.append(nc.dram_tensor("out", (B * S, D), F32, kind="ExternalOutput").ap())
    xattn_layer_kernel(nc, *args)
    r = run_bass_kernel_spmd(nc, [arrays], core_ids=[0])
    return r.results[0]["out"].reshape(B, S, D)
```
